# Optimizing a Trainium2 kernel written in Bass

```python
import numpy as np
import jax
import jax.numpy as jnp

def _softmax(x, axis=-1):
    return jax.nn.softmax(x, axis=axis)

def _gelu(x):
    return jax.nn.gelu(x, approximate=True)

def _silu(x):
    return jax.nn.silu(x)

def _sigmoid(x):
    return jax.nn.sigmoid(x)

def _layernorm(x, axis=-1, eps=1e-05):
    m = jnp.mean(x, axis=axis, keepdims=True)
    v = jnp.var(x, axis=axis, keepdims=True)
    return (x - m) / jnp.sqrt(v + eps)

def _scatter_add(tgt, idx, src, axis=0):
    return tgt.at[idx].add(src)

def _segment_sum(src, seg, n):
    return jax.ops.segment_sum(src, seg, n)
kernel_name = 'mk_adj_resnorm_d1_adj_r2_cd0312'

def setup_inputs(seed: int=0):
    np.random.seed(seed)
    _w = jnp.asarray

    def _rec_inputs():
        import jax
        import jax.numpy as jnp
        _gk = jax.random.key(seed)
        x = -0.000929 + 1 * jax.random.normal(jax.random.fold_in(_gk, 1), (2048, 256), jnp.float32)
        _a = jax.random.bernoulli(jax.random.fold_in(_gk, 2), 0.00390625, (2048, 2048))
        _af = _a.astype(jnp.float32)
        _af = _af * jax.random.uniform(jax.random.fold_in(_gk, 3), (2048, 2048), jnp.float32, 0.05, 5.22011)
        adj = _af
        return (x, adj)
    x, adj = _rec_inputs()

    def _L0_gnn_setup():
        import jax, jax.numpy as jnp
        import numpy as np
        N = 1024
        HID = 256
        H = 8
        key = jax.random.key(seed)
        ks = jax.random.split(key, 8)
        x = jax.random.normal(ks[0], (N, HID), dtype=jnp.float32)
        sp = jax.random.normal(ks[1], (N, N), dtype=jnp.float32)
        zero_mask = jax.random.uniform(ks[2], (N, N)) < 0.2
        spatial_encoding = jnp.where(zero_mask, 0.0, sp)
        edge_encoding = jax.random.normal(ks[3], (N, N), dtype=jnp.float32)
        s = 1.0 / np.sqrt(HID)
        Wq = jax.random.normal(ks[4], (HID, HID * H), dtype=jnp.float32) * s
        Wk = jax.random.normal(ks[5], (HID, HID * H), dtype=jnp.float32) * s
        Wv = jax.random.normal(ks[6], (HID, HID * H), dtype=jnp.float32) * s
        Wout = jax.random.normal(ks[7], (HID * H, HID), dtype=jnp.float32) * (1.0 / np.sqrt(HID * H))
        return {'x': x, 'spatial_encoding': spatial_encoding, 'edge_encoding': edge_encoding, 'Wq': Wq, 'Wk': Wk, 'Wv': Wv, 'Wout': Wout}
    _L0_gnn_all = _L0_gnn_setup()
    _L0_gnn_in = {k: v for k, v in _L0_gnn_all.items() if k in ('Wq', 'Wk', 'Wv', 'Wout')}
    del _L0_gnn_all
    return {'x': x, 'adj': adj, 'L0_gnn_Wq': _L0_gnn_in['Wq'], 'L0_gnn_Wk': _L0_gnn_in['Wk'], 'L0_gnn_Wv': _L0_gnn_in['Wv'], 'L0_gnn_Wout': _L0_gnn_in['Wout']}

def reference(x, adj, L0_gnn_Wq, L0_gnn_Wk, L0_gnn_Wv, L0_gnn_Wout):
    import jax
    import jax.numpy as jnp

    def _L0_gnn_ref(x, spatial_encoding, edge_encoding, Wq, Wk, Wv, Wout):
        import jax, jax.numpy as jnp
        import numpy as np
        N = 1024
        HID = 256
        H = 8
        n, d = x.shape
        h = Wq.shape[1] // d
        scale = d ** (-0.5)
        q = (x @ Wq).reshape(h, n, d)
        k = (x @ Wk).reshape(h, n, d)
        v = (x @ Wv).reshape(h, n, d)
        a = jnp.einsum('hnd,hmd->hnm', q, k) * scale
        a = a + spatial_encoding + edge_encoding
        mask = spatial_encoding == 0.0
        a = jnp.where(mask, -1000000.0, a)
        a = jax.nn.softmax(a, axis=-1)
        a = jnp.where(mask, 0.0, a)
        out = jnp.einsum('hnm,hmd->hnd', a, v)
        out = out.transpose(1, 0, 2).reshape(n, h * d)
        return out @ Wout
    x = _layernorm(x + _L0_gnn_ref(x, adj, adj, L0_gnn_Wq, L0_gnn_Wk, L0_gnn_Wv, L0_gnn_Wout), axis=-1)
    return x

_drawn_inputs = setup_inputs


def setup_inputs(seed=0):
    import zlib

    import numpy as np

    out = dict(_drawn_inputs(seed))
    spreads = {}
    factors = {}
    for name, (base, spread) in spreads.items():
        noise = np.random.default_rng([zlib.crc32(name.encode()), seed]).standard_normal(out[name].shape)
        drawn = base * np.exp(spread * noise) if base else spread * noise
        out[name] = jnp.asarray(drawn.astype(out[name].dtype))
    for name, factor in factors.items():
        out[name] = (out[name] * factor).astype(out[name].dtype)
    return out
```

```python
from contextlib import ExitStack

import concourse.bass as bass
from concourse import mybir

F32 = mybir.dt.float32
F32R = mybir.dt.float32r
ALU = mybir.AluOpType
ACT = mybir.ActivationFunctionType
AX_X = mybir.AxisListType.X

P = 128
BANK = 512
HI, LO = 0, 1
BIG = 2.0 ** 100
FLOOR = -1.0e6
NO_FLOOR = -(2.0 ** 120)
LOWEST = -3.0e38
EPS = 1e-5


def graph_attention_layernorm(nc, x, adj, wq, wk, wv, wout, out):
    N, D = x.shape
    H = wq.shape[1] // D
    C = N // (N // H)
    R = N // H
    KC = D // P
    HALVES = R // P
    TILES = C * HALVES
    BANKS = N // BANK
    TPB = BANK // P
    SCALE = float(D) ** -0.5
    assert C == H and KC == 2 and HALVES == 2 and BANKS == 4 and BANK == KC * R

    with ExitStack() as ctx:
        def sem(name):
            return ctx.enter_context(nc.semaphore(name))

        def sbuf(name, shape, dt=F32, where=ctx):
            return where.enter_context(nc.sbuf_tensor(name, shape, dt))

        def scratch(name, shape, dt):
            return nc.dram_tensor(name, shape, dt, kind="Internal").ap()

        pieces = {name: scratch(name + "_split", [C, P, 2, KC, D], F32)
                  for name in ("wk", "xt", "wv", "wout", "wq")}
        m_dram = scratch("m_dram", [TILES, P, N], F32)

        y_acc = sbuf("y_acc", [P, TILES, D])
        ident = sbuf("ident", [P, P])
        count = sbuf("count", [P, TILES + 1])
        floor = sbuf("floor", [P, TILES + 1])

        bank = [ctx.enter_context(nc.psum_tensor(f"bank{b}", [P, BANK], F32)) for b in range(8)]
        score_bank, pt_bank, y_bank, proj_bank = bank[0:4], bank[4:6], bank[6], bank[7]

        ident_ready = sem("ident_ready")
        y_init = sem("y_init")

        prep = ExitStack()
        raw_names = ("wk", "xt", "wv", "wout", "wq")
        raw = {n: sbuf("raw_" + n, [P, KC * C, D], where=prep) for n in raw_names}
        SPLITS = 4
        split = sbuf("split", [P, SPLITS, 2, KC * D], F32R, where=prep)
        adj_in = sbuf("adj_in", [P, 3, N], where=prep)
        zero_mark = sbuf("zero_mark", [P, 2, N], where=prep)
        m_out = sbuf("m_out", [P, 2, N], where=prep)
        junk = sbuf("junk", [P, N], where=prep)
        row_tmp = sbuf("row_tmp", [P, 2, TILES], where=prep)
        ones = sbuf("ones", [P, P], where=prep)

        raw_loaded = {n: sem("raw_loaded_" + n) for n in raw_names}
        adj_loaded = [sem(f"adj_loaded{i}") for i in range(3)]
        marked = sem("marked")
        counted = sem("counted")
        m_built = sem("m_built")
        m_stored = [sem(f"m_stored{i}") for i in range(2)]
        xt_turned = sem("xt_turned")
        split_hi = sem("split_hi")
        split_lo = sem("split_lo")
        split_stored = [sem(f"split_stored{i}") for i in range(SPLITS)]
        ones_ready = sem("ones_ready")
        floor_step = sem("floor_step")

        order = [(n, i) for n in raw_names for i in range(C)]

        def raw_piece(name, i):
            if name == "wout" or name == "xt":
                return raw[name][:, KC * i:KC * i + KC, :]
            v = raw[name][:].rearrange("p a b -> p (a b)").rearrange("p (k n) -> p k n", k=KC)
            return v[:, :, i * D:(i + 1) * D]

        def raw_dst(name):
            if name == "wout" or name == "xt":
                return raw[name][:]
            return raw[name][:].rearrange("p a b -> p (a b)").rearrange("p (k n) -> p k n", k=KC)

        raw_src = {"wk": wk.rearrange("(k p) n -> p k n", p=P), "wq": wq.rearrange("(k p) n -> p k n", p=P),
                   "wv": wv.rearrange("(k p) n -> p k n", p=P), "wout": wout.rearrange("(a p) e -> p a e", p=P),
                   "xt": x.rearrange("(a p) e -> p a e", p=P)}
        adj_rows = adj.rearrange("(f p c) j -> c f p j", f=HALVES, c=C)
        x_tokens = x.rearrange("(f p c) e -> f p c e", f=HALVES, c=C)
        out_tokens = out.rearrange("(f p c) e -> f p c e", f=HALVES, c=C)
        y_tokens = y_acc[:].rearrange("p (c f) e -> p f c e", f=HALVES)

        with nc.Block() as block:
            @block.sync
            def _(sp):
                for n in raw_names[:2]:
                    sp.dma_start(raw_dst(n), raw_src[n]).then_inc(raw_loaded[n], 16)
                adj_next = 0
                for k, (name, i) in enumerate(order):
                    if k % 8 == 0 and k // 8 + 2 < 5:
                        n = raw_names[k // 8 + 2]
                        sp.dma_start(raw_dst(n), raw_src[n]).then_inc(raw_loaded[n], 16)
                    if adj_next < TILES and k * TILES >= adj_next * len(order):
                        t = adj_next
                        if t >= 3:
                            sp.wait_ge(m_built, t - 2)
                        sp.dma_start(adj_in[:, t % 3, :], adj_rows[t // 2, t % 2]).then_inc(adj_loaded[t % 3], 16)
                        adj_next += 1
                        if t >= 2:
                            sp.wait_ge(m_built, t - 1)
                            sp.dma_start(m_dram[t - 2], m_out[:, t % 2, :]).then_inc(m_stored[t % 2], 16)
                    sp.wait_ge(split_lo, k + 1)
                    sp.dma_start(pieces[name][i].rearrange("p s k d -> p s (k d)"),
                                 split[:, k % SPLITS].bitcast(F32)).then_inc(split_stored[k % SPLITS], 16)
                for t in range(TILES - 2, TILES):
                    sp.wait_ge(m_built, t + 1)
                    sp.dma_start(m_dram[t], m_out[:, t % 2, :]).then_inc(m_stored[t % 2], 16)
                for f in range(HALVES):
                    sp.dma_start(y_tokens[:, f], x_tokens[f]).then_inc(y_init, 16)
                sp.wait_ge(y_init, 32)
                for i in range(SPLITS):
                    sp.wait_ge(split_stored[i], 16 * (len(order) // SPLITS))
                for i in range(2):
                    sp.wait_ge(m_stored[i], 16 * (TILES // 2))

            @block.gpsimd
            def _(pool):
                nc.gpsimd.memset(ones[:], 1.0).then_inc(ones_ready, 1)
                pool.wait_ge(ones_ready, 1)
                nc.gpsimd.affine_select(out=ident[:], in_=ones[:], compare_op=ALU.is_equal, fill=0.0, base=0,
                                        pattern=[[-1, P]], channel_multiplier=1).then_inc(ident_ready, 1)
                for t in range(TILES):
                    pool.wait_ge(adj_loaded[t % 3], 16 * (t // 3 + 1))
                    if t >= 2:
                        pool.wait_ge(m_built, t - 1)
                        pool.wait_ge(counted, t - 1)
                    nc.gpsimd.tensor_scalar(zero_mark[:, t % 2, :], adj_in[:, t % 3, :], 0.0, -BIG,
                                            ALU.is_equal, ALU.mult).then_inc(marked, 1)

            @block.scalar
            def _(act):
                def split_piece(k):
                    name, i = order[k]
                    if name == "xt":
                        act.wait_ge(xt_turned, i + 1)
                        src = score_bank[i % 4][:]
                    else:
                        act.wait_ge(raw_loaded[name], 16)
                        src = raw_piece(name, i)
                    if k >= SPLITS:
                        act.wait_ge(split_stored[k % SPLITS], 16 * (k // SPLITS))
                    dst = split[:, k % SPLITS, HI, :]
                    if name != "xt":
                        dst = dst.rearrange("p (k d) -> p k d", k=KC)
                    nc.scalar.activation(dst, src, ACT.Copy).then_inc(split_hi, 1)

                for k in range(len(order)):
                    split_piece(k)
                    if (k * TILES) // len(order) != ((k + 1) * TILES) // len(order):
                        t = (k * TILES) // len(order)
                        act.wait_ge(marked, t + 1)
                        if t >= 1:
                            act.wait_ge(counted, t)
                        nc.scalar.activation(junk[:], zero_mark[:, t % 2, :], ACT.Copy, scale=-1.0 / BIG,
                                             accum_out=count[:, t:t + 1]).then_inc(counted, 1)

            @block.vector
            def _(dve):
                for k in range(len(order)):
                    name, i = order[k]
                    dve.wait_ge(split_hi, k + 1)
                    hi = split[:, k % SPLITS, HI, :].bitcast(F32)
                    lo = split[:, k % SPLITS, LO, :]
                    if name == "xt":
                        src = score_bank[i % 4][:]
                    else:
                        src = raw_piece(name, i)
                        hi = hi.rearrange("p (k d) -> p k d", k=KC)
                        lo = lo.rearrange("p (k d) -> p k d", k=KC)
                    nc.vector.tensor_tensor(lo, src, hi, ALU.subtract).then_inc(split_lo, 1)
                    if (k * TILES) // len(order) != ((k + 1) * TILES) // len(order):
                        t = (k * TILES) // len(order)
                        dve.wait_ge(marked, t + 1)
                        if t >= 2:
                            dve.wait_ge(m_stored[t % 2], 16 * (t // 2))
                        nc.vector.scalar_tensor_tensor(
                            out=m_out[:, t % 2, :].rearrange("p (c r) -> p c r", c=C),
                            in0=adj_in[:, t % 3, :].rearrange("p (r c) -> p c r", c=C), scalar=2.0,
                            in1=zero_mark[:, t % 2, :].rearrange("p (r c) -> p c r", c=C),
                            op0=ALU.mult, op1=ALU.add).then_inc(m_built, 1)
                dve.wait_ge(counted, TILES)
                nc.vector.tensor_scalar(row_tmp[:, 0, :], count[:, 0:TILES], 0.0, NO_FLOOR,
                                        ALU.is_equal, ALU.mult).then_inc(floor_step, 1)
                nc.vector.tensor_scalar(row_tmp[:, 1, :], count[:, 0:TILES], 0.0, FLOOR,
                                        ALU.is_gt, ALU.mult).then_inc(floor_step, 1)
                dve.wait_ge(floor_step, 2)
                nc.vector.tensor_tensor(floor[:, 0:TILES], row_tmp[:, 0, :], row_tmp[:, 1, :],
                                        ALU.add).then_inc(floor_step, 1)
                dve.wait_ge(floor_step, 3)
                nc.vector.tensor_copy(floor[:, TILES:TILES + 1], floor[:, 0:1]).then_inc(floor_step, 1)
                dve.wait_ge(floor_step, 4)

            @block.tensor
            def _(pe):
                pe.wait_ge(ident_ready, 1)
                pe.wait_ge(raw_loaded["xt"], 16)
                for i in range(H):
                    if i >= 4:
                        pe.wait_ge(split_lo, C + i - 3)
                    for kc in range(KC):
                        for rt in range(HALVES):
                            mm = nc.tensor.transpose(score_bank[i % 4][:, kc * R + rt * P:kc * R + (rt + 1) * P],
                                                     raw["xt"][:, HALVES * i + rt, kc * P:(kc + 1) * P], ident[:])
                    mm.then_inc(xt_turned, 1)
        prep.close()

        k_split = [[sbuf(f"k{par}_{'hl'[s]}", [P, KC, N], F32R) for s in (HI, LO)] for par in range(2)]
        v_split = [sbuf(f"v{par}", [P, TILES, 2, D], F32R) for par in range(2)]
        t_p = sbuf("t_p", [P, N])
        m_sb = sbuf("m_sb", [P, BANKS, BANK])
        PT_SLOTS = 3
        SLOT = [0, 1, 2, 0]
        pt = [sbuf(f"pt_{'hl'[s]}", [P, PT_SLOTS, BANK], F32R) for s in (HI, LO)]
        piece_bufs = {n: sbuf(n, [P, 2, KC, D], F32R) for n in ("w_q", "w_k", "w_v", "w_out", "xt_q", "xt_kv")}
        q_split = sbuf("q_split", [P, 2, KC, R], F32R)
        vt_split = sbuf("vt_split", [P, 2, KC, R], F32R)
        bank_max = sbuf("bank_max", [P, BANKS + 1])
        neg_max = sbuf("neg_max", [P, 1])
        row_sum = sbuf("row_sum", [P, 1])
        floor_exp = sbuf("floor_exp", [P, 1])
        denom = sbuf("denom", [P, 1])
        rdenom = sbuf("rdenom", [P, 1])
        bn = sbuf("bn", [P, HALVES, 6])
        mean_var = sbuf("mean_var", [P, TILES, 2])
        stat = sbuf("stat", [P, 6, TILES])

        loaded = {n: sem("loaded_" + n) for n in piece_bufs}
        m_loaded = [sem(f"m_loaded{b}") for b in range(BANKS)]
        q_done, k_done, vt_done, v_done = sem("q_done"), sem("k_done"), sem("vt_done"), sem("v_done")
        q_hi, k_hi, vt_hi, v_hi = sem("q_hi"), sem("k_hi"), sem("vt_hi"), sem("v_hi")
        q_lo, k_lo, vt_lo, v_lo = sem("q_lo"), sem("k_lo"), sem("vt_lo"), sem("v_lo")
        scores_done, scored = sem("scores_done"), sem("scored")
        floor_copied, max_ready, exp_done, floor_done = sem("floor_copied"), sem("max_ready"), sem("exp_done"), sem("floor_done")
        denom_ready, rdenom_ready = sem("denom_ready"), sem("rdenom_ready")
        turned, pt_hi, pt_lo = sem("turned"), sem("pt_hi"), sem("pt_lo")
        y_done, y_half, y_added = sem("y_done"), sem("y_half"), sem("y_added")
        bn_ready, mv_ready, ln_var, ln_std = sem("bn_ready"), sem("mv_ready"), sem("ln_var"), sem("ln_std")
        ln_step, normed, stored = sem("ln_step"), sem("normed"), sem("stored")

        def at(eng, value):
            return value if isinstance(value, int) else eng.snap(value)

        def heads(eng, block_steps, unroll_last=False):
            def head(par, h, has_next):
                if unroll_last and not has_next:
                    for c in range(C):
                        block_steps(par, h * C + c, c, has_next, c == C - 1)
                    return
                with eng.Fori(0, C - 1) as c:
                    block_steps(par, at(eng, h * C + c), c, has_next, False)
                block_steps(par, at(eng, h * C + (C - 1)), C - 1, has_next, True)
            with eng.Fori(0, (H - 2) // 2) as pair:
                for par in range(2):
                    head(par, at(eng, pair * 2 + par), True)
            head(0, H - 2, True)
            head(1, H - 1, False)


        with nc.Block() as block:
            @block.sync
            def _(sp):
                def load(buf, src):
                    sp.dma_start(piece_bufs[buf][:].bitcast(F32), src).then_inc(loaded[buf], 16)

                def load_m(b, tile):
                    sp.dma_start(m_sb[:, b, :], m_dram[tile][:, b * BANK:(b + 1) * BANK]).then_inc(m_loaded[b], 16)

                load("xt_kv", pieces["xt"][0])
                load("w_v", pieces["wv"][0])
                load("w_k", pieces["wk"][0])
                load("w_out", pieces["wout"][0])
                load("w_q", pieces["wq"][0])
                load("xt_q", pieces["xt"][0])
                for b in range(BANKS):
                    load_m(b, 0)
                for c in range(1, C):
                    sp.wait_ge(vt_done, c)
                    load("w_v", pieces["wv"][c])
                    sp.wait_ge(k_done, c)
                    load("w_k", pieces["wk"][c])
                sp.wait_ge(vt_done, C)
                sp.wait_ge(k_done, C)
                load("xt_kv", pieces["xt"][1])
                sp.wait_ge(loaded["xt_kv"], 32)
                load("w_k", pieces["wk"][0])
                sp.wait_ge(v_done, C)
                load("w_out", pieces["wout"][1])
                sp.wait_ge(loaded["w_out"], 32)
                load("w_v", pieces["wv"][0])
                sp.wait_ge(q_done, 1)
                load("w_q", pieces["wq"][1])
                for b in range(BANKS):
                    sp.wait_ge(scored, b + 1)
                    load_m(b, 1)

                def block_loads(n, c, h, has_next, more_q, next_xt, final=False):
                    s4 = at(sp, n * 8)
                    closes = isinstance(c, int) and c == C - 1
                    for b in range(BANKS):
                        if not final:
                            sp.wait_ge(scored, s4 + (5 + b))
                            load_m(b, 0 if closes else c * 2 + 2)
                    if more_q:
                        sp.wait_ge(q_done, n + 2)
                        if isinstance(c, int) and c == C - 2:
                            load("xt_q", pieces["xt"][h + 1])
                            sp.wait_ge(loaded["xt_q"], h * 16 + 32)
                        load("w_q", pieces["wq"][(c + 2) % C if isinstance(c, int) else c + 2])
                    if has_next and not closes:
                        sp.wait_ge(k_done, n + (C + 1))
                        load("w_k", pieces["wk"][c + 1])
                        sp.wait_ge(vt_done, n + (C + 1))
                        load("w_v", pieces["wv"][c + 1])
                    if has_next and closes and next_xt:
                        sp.wait_ge(k_done, n + (C + 1))
                        sp.wait_ge(vt_done, n + (C + 1))
                        load("xt_kv", pieces["xt"][h + 2])
                    for b in range(BANKS):
                        if not final:
                            sp.wait_ge(scored, s4 + (9 + b))
                            load_m(b, 1 if closes else c * 2 + 3)
                    if has_next and closes and next_xt:
                        sp.wait_ge(loaded["xt_kv"], h * 16 + 48)
                        load("w_k", pieces["wk"][0])
                        sp.wait_ge(v_done, n + (C + 1))
                        load("w_out", pieces["wout"][h + 2])
                        sp.wait_ge(loaded["w_out"], h * 16 + 48)
                        load("w_v", pieces["wv"][0])

                def head_loads(h, has_next, next_xt):
                    with sp.Fori(0, C - 2) as c:
                        block_loads(at(sp, h * C + c), c, h, has_next, True, next_xt)
                    block_loads(at(sp, h * C + (C - 2)), C - 2, h, has_next, has_next, next_xt)
                    if has_next:
                        block_loads(at(sp, h * C + (C - 1)), C - 1, h, has_next, True, next_xt)

                with sp.Fori(0, H - 2) as h:
                    head_loads(h, True, True)
                head_loads(H - 2, True, False)
                head_loads(H - 1, False, False)
                for c in range(0, C, 2):
                    sp.wait_ge(normed, HALVES * (c + 2))
                    for f in range(HALVES):
                        sp.dma_start(out_tokens[f][:, c:c + 2], y_tokens[:, f, c:c + 2]).then_inc(stored, 16)
                sp.wait_ge(stored, 16 * TILES // 2)

            @block.tensor
            def _(pe):
                TERMS = [(a, b, k) for k in range(KC) for a, b in ((HI, HI), (HI, LO), (LO, HI))]

                def project(dst, left, right):
                    for o in range(2):
                        for i, (a, b, k) in enumerate(TERMS):
                            mm = nc.tensor.matmul(dst[:, o * R:(o + 1) * R], left[:, a, k, o * P:(o + 1) * P],
                                                  right[:, b, k, :], start=(i == 0), stop=(i == len(TERMS) - 1))
                    return mm

                def scores(par, f, b):
                    for i, (a, kk, k) in enumerate(TERMS):
                        mm = nc.tensor.matmul(score_bank[b][:], q_split[:, a, k, f * P:(f + 1) * P],
                                              k_split[par][kk][:, k, b * BANK:(b + 1) * BANK],
                                              start=(i == 0), stop=(i == len(TERMS) - 1))
                    mm.then_inc(scores_done, 1)

                def turn(g):
                    for j in range(TPB):
                        mm = nc.tensor.transpose(pt_bank[g % 2][:, j * P:(j + 1) * P],
                                                 t_p[:, (TPB * g + j) * P:(TPB * g + j + 1) * P], ident[:])
                    mm.then_inc(turned, 1)

                def values(par, g):
                    for j in range(TPB):
                        v = v_split[par][:, TPB * g + j]
                        hi_v = (y_bank[:], pt[HI][:, SLOT[g], j * P:(j + 1) * P], v.rearrange("p s d -> p (s d)"))
                        lo_v = (y_bank[:, 0:D], pt[LO][:, SLOT[g], j * P:(j + 1) * P], v[:, HI])
                        if g == 0 and j == 0:
                            nc.tensor.matmul(*hi_v, start=True, stop=False)
                            mm = nc.tensor.matmul(*lo_v, start=False, stop=False)
                        else:
                            nc.tensor.matmul(*lo_v, start=False, stop=False)
                            mm = nc.tensor.matmul(*hi_v, start=False, stop=(g == BANKS - 1 and j == TPB - 1))
                    return mm

                pe.wait_ge(loaded["xt_kv"], 16)
                pe.wait_ge(loaded["w_out"], 16)

                def first_kv(c, wait_bank):
                    pe.wait_ge(loaded["w_v"], c * 16 + 16)
                    project(pt_bank[0], piece_bufs["w_v"], piece_bufs["xt_kv"]).then_inc(vt_done, 1)
                    pe.wait_ge(loaded["w_k"], c * 16 + 16)
                    if wait_bank:
                        pe.wait_ge(k_lo, c)
                    project(score_bank[0], piece_bufs["w_k"], piece_bufs["xt_kv"]).then_inc(k_done, 1)
                    pe.wait_ge(vt_lo, c + 1)
                    if wait_bank:
                        pe.wait_ge(v_lo, c)
                    project(proj_bank, vt_split, piece_bufs["w_out"]).then_inc(v_done, 1)
                first_kv(0, False)
                with pe.Fori(1, C) as c:
                    first_kv(c, True)
                pe.wait_ge(loaded["w_q"], 16)
                pe.wait_ge(loaded["xt_q"], 16)
                project(y_bank, piece_bufs["w_q"], piece_bufs["xt_q"]).then_inc(q_done, 1)
                pe.wait_ge(k_lo, C)
                pe.wait_ge(y_added, 1)
                for b in range(BANKS):
                    scores(0, 0, b)

                def step(par, f, n, has_next, closes):
                    s4 = at(pe, n * 8 + 4 * f)
                    s1 = n * 2 + f
                    has_scores = has_next or not (closes and f == 1)
                    has_q = f == 0 and (has_next or not closes)
                    for g in range(BANKS):
                        if g == 0:
                            pe.wait_ge(exp_done, s1 + 1)
                        if g >= 2:
                            pe.wait_ge(pt_lo, s4 + (g - 1))
                        turn(g)
                        if has_scores:
                            if g == 0 and f == 1:
                                pe.wait_ge(q_lo, n + 1)
                                if closes:
                                    pe.wait_ge(k_lo, n + (C + 1))
                            pe.wait_ge(scored, s4 + (g + 1))
                            scores(par if not (closes and f == 1) else 1 - par, 1 - f, g)
                        if g == 1:
                            pe.wait_ge(pt_lo, s4 + 1)
                            pe.wait_ge(y_added, s1 + 1)
                            if f == 0:
                                pe.wait_ge(v_lo, n + C if has_next else H * C)
                            values(par, 0)
                            if has_next and f == 1:
                                pe.wait_ge(loaded["w_v"], n * 16 + 16 * (C + 1))
                                pe.wait_ge(k_lo, n + (C + 1))
                                project(proj_bank, piece_bufs["w_v"], piece_bufs["xt_kv"]).then_inc(vt_done, 1)
                    if has_q:
                        pe.wait_ge(loaded["w_q"], n * 16 + 32)
                        if not has_next:
                            pe.wait_ge(q_lo, n)
                        project(proj_bank, piece_bufs["w_q"], piece_bufs["xt_q"]).then_inc(q_done, 1)
                    for g in (1, 2):
                        pe.wait_ge(pt_lo, s4 + (g + 1))
                        values(par, g)
                    if has_next and f == 0:
                        pe.wait_ge(loaded["w_k"], n * 16 + 16 * (C + 1))
                        pe.wait_ge(q_lo, n + 1)
                        project(proj_bank, piece_bufs["w_k"], piece_bufs["xt_kv"]).then_inc(k_done, 1)
                    if has_next and f == 1:
                        pe.wait_ge(vt_lo, n + (C + 1))
                        project(proj_bank, vt_split, piece_bufs["w_out"]).then_inc(v_done, 1)
                    pe.wait_ge(pt_lo, s4 + 4)
                    values(par, 3).then_inc(y_done, 1)

                def block_steps(par, n, c, has_next, closes):
                    for f in range(HALVES):
                        step(par, f, n, has_next, closes)

                heads(pe, block_steps)

            @block.scalar
            def _(act):
                def hi_of(done, value, dst, src, hi_sem, scale=1.0):
                    act.wait_ge(done, value)
                    nc.scalar.activation(dst, src, ACT.Copy, scale=scale).then_inc(hi_sem, 1)

                def k_part(par, c):
                    return k_split[par][HI][:, :, bass.ds(c * R, R)]

                def v_part(par, c):
                    return v_split[par][:, bass.ds(c * HALVES, HALVES), HI, :]

                def halves(bank_ap):
                    return bank_ap[:].rearrange("p (o r) -> p o r", o=2)

                def exp_tile(value):
                    act.wait_ge(max_ready, value)
                    nc.scalar.activation(t_p[:], t_p[:], ACT.Exp, bias=neg_max[:], scale=1.0,
                                         accum_out=row_sum[:]).then_inc(exp_done, 1)
                    nc.scalar.activation(floor_exp[:], bank_max[:, BANKS:BANKS + 1], ACT.Exp, bias=neg_max[:],
                                         scale=1.0).then_inc(floor_done, 1)

                with act.Fori(0, C) as c:
                    hi_of(vt_done, c + 1, vt_split[:, HI], halves(pt_bank[0]), vt_hi)
                    hi_of(k_done, c + 1, k_part(0, c), halves(score_bank[0]), k_hi)
                    hi_of(v_done, c + 1, v_part(0, c), halves(proj_bank), v_hi)
                hi_of(q_done, 1, q_split[:, HI], halves(y_bank), q_hi, SCALE)
                exp_tile(1)

                def block_steps(par, n, c, has_next, closes):
                    for f in range(HALVES):
                        s4 = at(act, n * 8 + 4 * f)
                        for g in range(BANKS):
                            hi_of(turned, s4 + (g + 1), pt[HI][:, SLOT[g], :], pt_bank[g % 2][:], pt_hi)
                            if g == 1 and f == 1 and has_next:
                                hi_of(vt_done, n + (C + 1), vt_split[:, HI], halves(proj_bank), vt_hi)
                        if f == 0 and (has_next or not closes):
                            hi_of(q_done, n + 2, q_split[:, HI], halves(proj_bank), q_hi, SCALE)
                        if has_next or not (closes and f == 1):
                            exp_tile(n * 2 + (f + 2))
                        if has_next and f == 0:
                            hi_of(k_done, n + (C + 1), k_part(1 - par, c), halves(proj_bank), k_hi)
                        if has_next and f == 1:
                            hi_of(v_done, n + (C + 1), v_part(1 - par, c), halves(proj_bank), v_hi)
                heads(act, block_steps)

                act.wait_ge(ln_var, 1)
                nc.scalar.activation(stat[:, 1, :], stat[:, 0, :], ACT.Sqrt).then_inc(ln_std, 1)

            @block.vector
            def _(dve):
                def lo_of(hi_sem, value, dst, hi, src, lo_sem, scale=None):
                    dve.wait_ge(hi_sem, value)
                    if scale is None:
                        ins = nc.vector.tensor_tensor(dst, src, hi, ALU.subtract)
                    else:
                        ins = nc.vector.scalar_tensor_tensor(out=dst, in0=src, scalar=scale, in1=hi,
                                                             op0=ALU.mult, op1=ALU.subtract)
                    ins.then_inc(lo_sem, 1)

                def k_part(par, s, c):
                    return k_split[par][s][:, :, bass.ds(c * R, R)]

                def v_part(par, s, c):
                    return v_split[par][:, bass.ds(c * HALVES, HALVES), s, :]

                def halves(bank_ap):
                    return bank_ap[:].rearrange("p (o r) -> p o r", o=2)

                def score(b, tile):
                    if b == 0:
                        nc.vector.tensor_copy(bank_max[:, BANKS:BANKS + 1],
                                              floor[:, bass.ds(tile, 1)]).then_inc(floor_copied, 1)
                    nc.vector.tensor_tensor_reduce(out=t_p[:, b * BANK:(b + 1) * BANK], in0=score_bank[b][:],
                                                   in1=m_sb[:, b, :], scale=1.0,
                                                   scalar=LOWEST, op0=ALU.add,
                                                   op1=ALU.max, accum_out=bank_max[:, b:b + 1]).then_inc(scored, 1)

                def row_max(value, floors):
                    dve.wait_ge(floor_copied, floors)
                    dve.wait_ge(scored, value)
                    nc.vector.tensor_reduce(neg_max[:], bank_max[:], AX_X, ALU.max, negate=True).then_inc(max_ready, 1)

                with dve.Fori(0, C) as c:
                    lo_of(vt_hi, c + 1, vt_split[:, LO], vt_split[:, HI].bitcast(F32), halves(pt_bank[0]), vt_lo)
                    lo_of(k_hi, c + 1, k_part(0, LO, c), k_part(0, HI, c).bitcast(F32), halves(score_bank[0]), k_lo)
                    lo_of(v_hi, c + 1, v_part(0, LO, c), v_part(0, HI, c).bitcast(F32), halves(proj_bank), v_lo)
                lo_of(q_hi, 1, q_split[:, LO], q_split[:, HI].bitcast(F32), halves(y_bank), y_added, SCALE)
                for b in range(BANKS):
                    dve.wait_ge(scores_done, b + 1)
                    dve.wait_ge(m_loaded[b], 16)
                    score(b, 0)
                row_max(BANKS, 1)

                def step(par, f, n, c, has_next, closes):
                    s4 = at(dve, n * 8 + 4 * f)
                    s1 = at(dve, n * 2 + f)
                    has_scores = has_next or not (closes and f == 1)
                    dve.wait_ge(exp_done, s1 + 1)
                    dve.wait_ge(floor_done, s1 + 1)
                    nc.vector.scalar_tensor_tensor(out=denom[:], in0=floor_exp[:],
                                                   scalar=count[:, bass.ds(c * HALVES + f, 1)], in1=row_sum[:],
                                                   op0=ALU.mult, op1=ALU.add).then_inc(denom_ready, 1)
                    dve.wait_ge(denom_ready, s1 + 1)
                    nc.vector.reciprocal(rdenom[:], denom[:]).then_inc(rdenom_ready, 1)
                    for g in range(BANKS):
                        if has_scores:
                            dve.wait_ge(scores_done, s4 + (5 + g))
                            dve.wait_ge(m_loaded[g], s1 * 16 + 32)
                        lo_of(pt_hi, s4 + (g + 1), pt[LO][:, SLOT[g], :], pt[HI][:, SLOT[g], :].bitcast(F32),
                              pt_bank[g % 2][:], pt_lo)
                        if has_scores:
                            score(g, c * HALVES + (f + 1))
                        if g == 1 and f == 1 and has_next:
                            lo_of(vt_hi, n + (C + 1), vt_split[:, LO], vt_split[:, HI].bitcast(F32),
                                  halves(proj_bank), vt_lo)
                    if has_scores:
                        row_max(s4 + 8, s1 + 2)
                    if f == 0 and (has_next or not closes):
                        lo_of(q_hi, n + 2, q_split[:, LO], q_split[:, HI].bitcast(F32), halves(proj_bank), q_lo, SCALE)
                    if has_next and f == 0:
                        lo_of(k_hi, n + (C + 1), k_part(1 - par, LO, c), k_part(1 - par, HI, c).bitcast(F32),
                              halves(proj_bank), k_lo)
                    if has_next and f == 1:
                        lo_of(v_hi, n + (C + 1), v_part(1 - par, LO, c), v_part(1 - par, HI, c).bitcast(F32),
                              halves(proj_bank), v_lo)
                    tile = c * HALVES + f
                    y = y_acc[:, tile, :] if isinstance(tile, int) else \
                        y_acc[:, bass.ds(tile, 1), :].rearrange("p a d -> p (a d)")
                    dve.wait_ge(y_done, s1 + 1)
                    dve.wait_ge(rdenom_ready, s1 + 1)
                    nc.vector.scalar_tensor_tensor(out=y, in0=y_bank[:, 0:D], scalar=rdenom[:], in1=y,
                                                   op0=ALU.mult, op1=ALU.add).then_inc(y_half, 1)
                    dve.wait_ge(y_half, s1 + 1)
                    nc.vector.scalar_tensor_tensor(out=y, in0=y_bank[:, D:2 * D], scalar=rdenom[:], in1=y,
                                                   op0=ALU.mult, op1=ALU.add).then_inc(y_added, 1)
                    if not has_next:
                        dve.wait_ge(y_added, s1 + 2)
                        nc.vector.bn_stats(bn[:, f, :], y).then_inc(bn_ready, 1)
                        tile = c * HALVES + f
                        dve.wait_ge(bn_ready, tile + 1)
                        nc.vector.bn_aggr(mean_var[:, tile, :], bn[:, f, :]).then_inc(mv_ready, 1)

                def block_steps(par, n, c, has_next, closes):
                    for f in range(HALVES):
                        step(par, f, n, c, has_next, closes)
                heads(dve, block_steps, unroll_last=True)

                dve.wait_ge(mv_ready, TILES)
                nc.vector.tensor_scalar(stat[:, 0, :], mean_var[:, :, 1], EPS, None, ALU.add).then_inc(ln_var, 1)
                dve.wait_ge(ln_std, 1)
                nc.vector.reciprocal(stat[:, 2, :], stat[:, 1, :]).then_inc(ln_step, 1)
                dve.wait_ge(ln_step, 1)
                nc.vector.tensor_tensor(stat[:, 3, :], stat[:, 2, :], stat[:, 2, :], ALU.mult).then_inc(ln_step, 1)
                dve.wait_ge(ln_step, 2)
                nc.vector.tensor_tensor(stat[:, 4, :], stat[:, 3, :], stat[:, 0, :], ALU.mult).then_inc(ln_step, 1)
                dve.wait_ge(ln_step, 3)
                nc.vector.tensor_scalar(stat[:, 3, :], stat[:, 4, :], -0.5, 1.5, ALU.mult,
                                        ALU.add).then_inc(ln_step, 1)
                dve.wait_ge(ln_step, 4)
                nc.vector.tensor_tensor(stat[:, 5, :], stat[:, 3, :], stat[:, 2, :], ALU.mult).then_inc(ln_step, 1)
                dve.wait_ge(ln_step, 5)
                for t in range(TILES):
                    nc.vector.tensor_scalar(y_acc[:, t, :], y_acc[:, t, :], mean_var[:, t, 0:1], stat[:, 5, t:t + 1],
                                            ALU.subtract, ALU.mult).then_inc(normed, 1)


_INS = ["x", "adj", "L0_gnn_Wq", "L0_gnn_Wk", "L0_gnn_Wv", "L0_gnn_Wout"]


def kernel(**inputs):
    import numpy as _np
    import concourse.bacc as _bacc
    from concourse.bass_utils import run_bass_kernel_spmd as _run

    nc = _bacc.Bacc("TRN2", target_bir_lowering=False, num_devices=1)
    arrays, args = {}, []
    for name in _INS:
        a = _np.ascontiguousarray(inputs[name])
        arrays[f"in_{name}_dram"] = a
        args.append(nc.dram_tensor(f"in_{name}_dram", a.shape, mybir.dt.from_np(a.dtype), kind="ExternalInput").ap())
    args.append(nc.dram_tensor("out_0_dram", inputs["x"].shape, F32, kind="ExternalOutput").ap())
    graph_attention_layernorm(nc, *args)
    r = _run(nc, [arrays], core_ids=[0])
    return r.results[0]["out_0_dram"]
```

```python
from contextlib import ExitStack

import concourse.bass as bass
from concourse import mybir

F32 = mybir.dt.float32
F32R = mybir.dt.float32r
ALU = mybir.AluOpType
ACT = mybir.ActivationFunctionType
AX_X = mybir.AxisListType.X

P = 128
BANK = 512
HI, LO = 0, 1
BIG = 2.0 ** 100
FLOOR = -1.0e6
NO_FLOOR = -(2.0 ** 120)
LOWEST = -3.0e38
EPS = 1e-5


def columns(w, c, size):
    return w.rearrange("(k p) n -> p k n", p=P)[:, :, bass.ds(c * size, size)]


def graph_attention_layernorm(nc, x, adj, wq, wk, wv, wout, out):
    N, D = x.shape
    H = wq.shape[1] // D
    C = N // (N // H)
    R = N // H
    KC = D // P
    HALVES = R // P
    TILES = C * HALVES
    BANKS = N // BANK
    TPB = BANK // P
    SCALE = float(D) ** -0.5
    assert C == H and KC == 2 and HALVES == 2 and BANKS == 4 and BANK == KC * R

    with ExitStack() as ctx:
        def sem(name):
            return ctx.enter_context(nc.semaphore(name))

        def sbuf(name, shape, dt=F32, where=ctx):
            return where.enter_context(nc.sbuf_tensor(name, shape, dt))

        m_dram = nc.dram_tensor("m_dram", [TILES, P, N], F32, kind="Internal").ap()

        y_acc = sbuf("y_acc", [P, TILES, D])
        ident = sbuf("ident", [P, P])
        k0 = sbuf("k0", [P, 2, KC, N], F32R)
        v0 = sbuf("v0", [P, TILES, 2, D], F32R)
        q_split = sbuf("q_split", [P, 2, KC, R], F32R)
        vt_split = sbuf("vt_split", [P, 2, KC, R], F32R)
        w_split = {n: sbuf(n, [P, 2, KC, D], F32R) for n in ("w_q", "w_k", "w_v")}
        before = ExitStack()
        raw_x, raw_wout = [], None
        for what in ("x0", "x1", "wout"):
            sbuf("high_of_" + what, [P, KC, D], where=before)
            raw_wout = sbuf("raw_" + what, [P, KC, D], where=before)
            raw_x.append(raw_wout)
        raw_x.pop()
        before.close()
        xt = [sbuf(f"xt{par}", [P, 2, KC, D], F32R) for par in range(2)]
        w_out = sbuf("w_out", [P, 2, KC, D], F32R)
        raw = {n: sbuf("raw_" + n, [P, KC, D]) for n in ("w_q", "w_k", "w_v")}
        m_sb = sbuf("m_sb", [P, BANKS, BANK])
        t_p = sbuf("t_p", [P, N])
        zero_mark = sbuf("zero_mark", [P, BANK], mybir.dt.uint8)
        small = sbuf("small", [P, 160])

        taken = [0]

        def part_of_small(n):
            taken[0] += n
            return small[:, taken[0] - n:taken[0]]

        bank_max = part_of_small(BANKS + 1)
        neg_max, row_sum, floor_exp, denom, rdenom = (part_of_small(1) for _ in range(5))
        chunk_count = part_of_small(BANKS)
        count = part_of_small(TILES)
        no_mask = part_of_small(TILES + 1)
        bn = part_of_small(6)
        mean_var = part_of_small(2 * TILES).rearrange("p (t s) -> p t s", s=2)
        var_eps, std, rstd, newton = (part_of_small(TILES) for _ in range(4))

        bank = [ctx.enter_context(nc.psum_tensor(f"bank{b}", [P, BANK], F32)) for b in range(8)]
        score_bank, pt_bank, y_bank, proj_bank = bank[0:4], bank[4:6], bank[6], bank[7]

        x_loaded, xt_turned, xt_hi, xt_lo = sem("x_loaded"), sem("xt_turned"), sem("xt_hi"), sem("xt_lo")
        wout_loaded, wout_hi, wout_lo = sem("wout_loaded"), sem("wout_hi"), sem("wout_lo")
        y_init = sem("y_init")
        m_loaded = [sem(f"m_loaded{b}") for b in range(BANKS)]
        q_done, k_done, vt_done, v_done = sem("q_done"), sem("k_done"), sem("vt_done"), sem("v_done")
        q_hi, k_hi, vt_hi, v_hi = sem("q_hi"), sem("k_hi"), sem("vt_hi"), sem("v_hi")
        q_lo, k_lo, vt_lo, v_lo = sem("q_lo"), sem("k_lo"), sem("vt_lo"), sem("v_lo")
        scores_done, scored = sem("scores_done"), sem("scored")
        w_hi = {n: sem("hi_" + n) for n in raw}
        w_lo = {n: sem("lo_" + n) for n in raw}
        raw_loaded = {n: sem("loaded_raw_" + n) for n in raw}
        adj_loaded = [sem(f"adj_loaded{i}") for i in range(BANKS)]
        marked, m_chunk, counted, m_stored = sem("marked"), sem("m_chunk"), sem("counted"), sem("m_stored")
        floor_copied, max_ready, exp_done, floor_done = (sem("floor_copied"), sem("max_ready"), sem("exp_done"),
                                                         sem("floor_done"))
        denom_ready, rdenom_ready = sem("denom_ready"), sem("rdenom_ready")
        floors_ready = sem("floors_ready")
        turned, pt_hi, pt_lo = sem("turned"), sem("pt_hi"), sem("pt_lo")
        y_done, y_half, y_added = sem("y_done"), sem("y_half"), sem("y_added")

        adj_rows = adj.rearrange("(f p c) j -> c f p j", f=HALVES, c=C)
        x_tokens = x.rearrange("(f p c) e -> f p c e", f=HALVES, c=C)
        out_tokens = out.rearrange("(f p c) e -> f p c e", f=HALVES, c=C)
        y_tokens = y_acc[:].rearrange("p (c f) e -> p f c e", f=HALVES)

        TERMS = [(a, b, k) for k in range(KC) for a, b in ((HI, HI), (HI, LO), (LO, HI))]

        def project(dst, left, right):
            for o in range(2):
                for i, (a, b, k) in enumerate(TERMS):
                    mm = nc.tensor.matmul(dst[:, o * R:(o + 1) * R], left[:, a, k, o * P:(o + 1) * P],
                                          right[:, b, k, :], start=(i == 0), stop=(i == len(TERMS) - 1))
            return mm

        def scores(k_both, f, b):
            for i, (a, kk, k) in enumerate(TERMS):
                mm = nc.tensor.matmul(score_bank[b][:], q_split[:, a, k, f * P:(f + 1) * P],
                                      k_both[:, kk, k, b * BANK:(b + 1) * BANK],
                                      start=(i == 0), stop=(i == len(TERMS) - 1))
            mm.then_inc(scores_done, 1)

        def turn_x(pe, par, bank_of_x, loads):
            pe.wait_ge(x_loaded, loads)
            for kc in range(KC):
                for f in range(HALVES):
                    mm = nc.tensor.transpose(bank_of_x[:, kc * R + f * P:kc * R + (f + 1) * P],
                                             raw_x[par][:, f, kc * P:(kc + 1) * P], ident[:])
            mm.then_inc(xt_turned, 1)

        def hi_of(act, done, value, dst, src, hi_sem, scale=1.0):
            act.wait_ge(done, value)
            nc.scalar.activation(dst, src, ACT.Copy, scale=scale).then_inc(hi_sem, 1)

        def exp_tile(act, value):
            act.wait_ge(max_ready, value)
            nc.scalar.activation(t_p[:], t_p[:], ACT.Exp, bias=neg_max, scale=1.0,
                                 accum_out=row_sum).then_inc(exp_done, 1)
            nc.scalar.activation(floor_exp, bank_max[:, BANKS:BANKS + 1], ACT.Exp, bias=neg_max,
                                 scale=1.0).then_inc(floor_done, 1)

        def hi_w(act, name, src, loads_sem, loads, used, uses):
            act.wait_ge(loads_sem, loads)
            if uses is not None:
                act.wait_ge(used, uses)
            nc.scalar.activation(w_split[name][:, HI], src, ACT.Copy).then_inc(w_hi[name], 1)

        def hi_wout(act, pieces):
            act.wait_ge(wout_loaded, pieces * 16)
            nc.scalar.activation(w_out[:, HI], raw_wout[:], ACT.Copy).then_inc(wout_hi, 1)

        def lo_w(pool, name, src, value):
            pool.wait_ge(w_hi[name], value)
            nc.gpsimd.tensor_tensor(w_split[name][:, LO], src, w_split[name][:, HI].bitcast(F32),
                                    ALU.subtract).then_inc(w_lo[name], 1)

        def lo_wout(pool, value):
            pool.wait_ge(wout_hi, value)
            nc.gpsimd.tensor_tensor(w_out[:, LO], raw_wout[:], w_out[:, HI].bitcast(F32),
                                    ALU.subtract).then_inc(wout_lo, 1)

        def lo_of(dve, hi_sem, value, dst, hi, src, lo_sem, scale=None):
            dve.wait_ge(hi_sem, value)
            if scale is None:
                ins = nc.vector.tensor_tensor(dst, src, hi.bitcast(F32), ALU.subtract)
            else:
                ins = nc.vector.scalar_tensor_tensor(out=dst, in0=src, scalar=scale, in1=hi.bitcast(F32),
                                                     op0=ALU.mult, op1=ALU.subtract)
            ins.then_inc(lo_sem, 1)

        def score(b, tile):
            if b == 0:
                nc.vector.tensor_scalar(bank_max[:, BANKS:BANKS + 1], no_mask[:, bass.ds(tile, 1)], FLOOR, None,
                                        ALU.add).then_inc(floor_copied, 1)
            nc.vector.tensor_tensor_reduce(out=t_p[:, b * BANK:(b + 1) * BANK], in0=score_bank[b][:],
                                           in1=m_sb[:, b, :], scale=2.0, scalar=LOWEST, op0=ALU.add,
                                           op1=ALU.max, accum_out=bank_max[:, b:b + 1]).then_inc(scored, 1)

        def row_max(dve, value, floors):
            dve.wait_ge(floor_copied, floors)
            dve.wait_ge(scored, value)
            nc.vector.tensor_reduce(neg_max, bank_max, AX_X, ALU.max, negate=True).then_inc(max_ready, 1)

        def m_made(v):
            first = {0: m_sb[:].rearrange("p b k -> p (b k)"), 2: t_p[:]}
            return first.get(v, m_build[:]) if isinstance(v, int) else m_build[:]

        def mark_chunk(dve, v, q):
            s4 = v * BANKS if isinstance(v, int) else dve.snap(v * BANKS)
            dve.wait_ge(adj_loaded[q], v * 16 + 16)
            if not (isinstance(v, int) and v == 0 and q == 0):
                dve.wait_ge(m_chunk, s4 + q if q else s4)
            nc.vector.tensor_scalar(zero_mark[:], adj_chunk[q][:], 0.0, None, ALU.is_equal, ALU.add,
                                    accum_out=chunk_count[:, q:q + 1]).then_inc(marked, 1)

        def put_chunk(dve, v, q):
            rows = BANK // C
            s4 = v * BANKS if isinstance(v, int) else dve.snap(v * BANKS)
            dve.wait_ge(marked, s4 + (q + 1))
            if q == 0 and isinstance(v, int) and v == 3:
                dve.wait_ge(m_stored, 16 * 2)
            if q == 0 and not (isinstance(v, int) and v <= 3):
                dve.wait_ge(m_stored, v * 16)
            nc.vector.scalar_tensor_tensor(
                out=m_made(v).rearrange("p (c r) -> p c r", c=C)[:, :, q * rows:(q + 1) * rows],
                in0=zero_mark[:].rearrange("p (r c) -> p c r", c=C), scalar=-BIG,
                in1=adj_chunk[q][:].rearrange("p (r c) -> p c r", c=C),
                op0=ALU.mult, op1=ALU.add).then_inc(m_chunk, 1)
            if q == BANKS - 1:
                nc.vector.tensor_reduce(count[:, bass.ds(v, 1)], chunk_count, AX_X, ALU.add).then_inc(counted, 1)
                dve.wait_ge(counted, v + 1)
                nc.vector.tensor_scalar(no_mask[:, bass.ds(v, 1)], count[:, bass.ds(v, 1)], 0.0, NO_FLOOR,
                                        ALU.is_equal, ALU.mult).then_inc(floors_ready, 1)

        def k_part(k_both, part, c):
            return k_both[:, part, :, bass.ds(c * R, R)]

        def v_part(v_both, part, c):
            return v_both[:, bass.ds(c * HALVES, HALVES), part, :]

        def halves(bank_ap):
            return bank_ap[:].rearrange("p (o r) -> p o r", o=2)

        def rows_of(w, h):
            return w[bass.ds(h * R, R), :].rearrange("(a p) e -> p a e", p=P)

        def load_x(sp, par, h):
            sp.dma_start(raw_x[par][:], rows_of(x, h)).then_inc(x_loaded, 16)

        def load_wout(sp, h):
            sp.dma_start(raw_wout[:], rows_of(wout, h)).then_inc(wout_loaded, 16)

        def load_raw(sp, name, c):
            w = {"w_q": wq, "w_k": wk, "w_v": wv}[name]
            sp.dma_start(raw[name][:], columns(w, c, D)).then_inc(raw_loaded[name], 16)

        def load_adj(sp, q, c, f):
            sp.dma_start(adj_chunk[q][:], adj_rows[c, f][:, q * BANK:(q + 1) * BANK]).then_inc(adj_loaded[q], 16)

        def store_m(sp, tile):
            sp.dma_start(m_dram[tile], m_made(tile)).then_inc(m_stored, 16)

        def load_m(sp, b, tile):
            sp.dma_start(m_sb[:, b, :], m_dram[tile][:, b * BANK:(b + 1) * BANK]).then_inc(m_loaded[b], 16)

        early = ExitStack()
        places, adj_chunk = [], []

        def place():
            places.append(sbuf(f"place{len(places)}", [P, KC, D], where=early))

        for row in range(2 * KC):
            for _ in range(N // BANK - 1):
                place()
            adj_chunk.append(sbuf(f"adj_chunk{row}", [P, BANK], where=early))
        for _ in range(TILES - BANKS):
            place()
        m_build = sbuf("m_build", [P, N], where=early)
        early.close()
        k1 = sbuf("k1", [P, 2, KC, N], F32R)
        v1 = sbuf("v1", [P, TILES, 2, D], F32R)
        PT_SLOTS = 2
        pt = [sbuf(f"pt_{'hl'[part]}", [P, PT_SLOTS, BANK], F32R) for part in (HI, LO)]

        def pt_group(part, g, last_head):
            if last_head and g == BANKS - 1:
                return k0[:, part, 0, 0:BANK]
            return pt[part][:, g % PT_SLOTS, :]

        EARLY_TILES = 4

        early_w = {("w_v", c): places[2 * c] for c in range(C)}
        early_w.update({("w_k", c): places[2 * c + 1] for c in range(C)})
        early_w["w_q", 0] = places[2 * C]
        early_loaded = {key: sem("loaded_early_%s%d" % key) for key in early_w}
        ident_ready, ident_filled, no_mask_copied = sem("ident_ready"), sem("ident_filled"), sem("no_mask_copied")
        w_src = {"w_k": wk, "w_q": wq, "w_v": wv}
        k_bank, vt_banks, x_banks, v_bank = score_bank[0], pt_bank, score_bank[1:3], proj_bank

        with nc.Block() as block:
            @block.sync
            def _(sp):
                def load_early(name, c):
                    sp.dma_start(early_w[name, c][:], columns(w_src[name], c, D)).then_inc(early_loaded[name, c], 16)

                load_x(sp, 0, 0)
                load_early("w_v", 0)
                load_early("w_k", 0)
                load_wout(sp, 0)
                load_early("w_v", 1)
                for q in range(BANKS // 2):
                    load_adj(sp, q, 0, 0)
                load_early("w_k", 1)
                sp.wait_ge(x_loaded, 16)
                load_x(sp, 1, 1)
                for q in range(BANKS // 2, BANKS):
                    load_adj(sp, q, 0, 0)
                for c in range(2, C):
                    load_early("w_v", c)
                    load_early("w_k", c)
                load_early("w_q", 0)
                load_raw(sp, "w_q", 1)
                load_raw(sp, "w_k", 0)
                load_raw(sp, "w_v", 0)
                for t in range(EARLY_TILES):
                    for q in range(BANKS):
                        sp.wait_ge(m_chunk, t * BANKS + q + 1)
                        load_adj(sp, q, (t + 1) // 2, (t + 1) % 2)
                    if t:
                        sp.wait_ge(m_stored, 16 * t)
                    store_m(sp, t)
                sp.wait_ge(v_done, C)
                load_wout(sp, 1)
                sp.wait_ge(m_stored, 16 * 2)
                for b in range(BANKS):
                    sp.wait_ge(scored, b + 1)
                    load_m(sp, b, 1)
                for f in range(HALVES):
                    sp.dma_start(y_tokens[:, f], x_tokens[f]).then_inc(y_init, 16)

            @block.gpsimd
            def _(pool):
                nc.gpsimd.memset(t_p[:, 0:P], 1.0).then_inc(ident_filled, 1)
                pool.wait_ge(ident_filled, 1)
                nc.gpsimd.affine_select(out=ident[:], in_=t_p[:, 0:P], compare_op=ALU.is_equal, fill=0.0, base=0,
                                        pattern=[[-1, P]], channel_multiplier=1).then_inc(ident_ready, 1)
                lo_w(pool, "w_v", early_w["w_v", 0][:], 1)
                lo_w(pool, "w_k", early_w["w_k", 0][:], 1)
                lo_w(pool, "w_v", early_w["w_v", 1][:], 2)
                lo_wout(pool, 1)
                for c in range(1, C):
                    lo_w(pool, "w_k", early_w["w_k", c][:], c + 1)
                    if c + 1 < C:
                        lo_w(pool, "w_v", early_w["w_v", c + 1][:], c + 2)
                lo_w(pool, "w_q", early_w["w_q", 0][:], 1)

            @block.scalar
            def _(act):
                def hi_early(name, c, used):
                    hi_w(act, name, early_w[name, c][:], early_loaded[name, c], 16, used, c if c else None)

                def hi_x(c):
                    hi_of(act, xt_turned, c + 1, xt[c][:, HI], halves(x_banks[c]), xt_hi)

                hi_x(0)
                hi_early("w_v", 0, vt_done)
                hi_early("w_k", 0, k_done)
                hi_early("w_v", 1, vt_done)
                hi_of(act, vt_done, 1, vt_split[:, HI], halves(vt_banks[0]), vt_hi)
                hi_wout(act, 1)
                for c in range(C):
                    hi_of(act, k_done, c + 1, k_part(k0, HI, c), halves(k_bank), k_hi)
                    if c + 1 < C:
                        hi_early("w_k", c + 1, k_done)
                    if c + 2 < C:
                        hi_early("w_v", c + 2, vt_done)
                    act.wait_ge(v_done, c + 1)
                    if c + 1 < C:
                        hi_of(act, vt_done, c + 2, vt_split[:, HI], halves(vt_banks[(c + 1) % 2]), vt_hi)
                    hi_of(act, v_done, c + 1, v_part(v0, HI, c), halves(v_bank), v_hi)
                    if c == 1:
                        hi_x(1)
                    if c == C - 2:
                        hi_early("w_q", 0, q_done)
                hi_of(act, q_done, 1, q_split[:, HI], halves(y_bank), q_hi, SCALE / 2)
                exp_tile(act, 1)

            @block.vector
            def _(dve):
                def lo_x(c):
                    lo_of(dve, xt_hi, c + 1, xt[c][:, LO], xt[c][:, HI], halves(x_banks[c]), xt_lo)

                lo_x(0)
                lo_of(dve, vt_hi, 1, vt_split[:, LO], vt_split[:, HI], halves(vt_banks[0]), vt_lo)
                for c in range(C):
                    lo_of(dve, k_hi, c + 1, k_part(k0, LO, c), k_part(k0, HI, c), halves(k_bank), k_lo)
                    mark_chunk(dve, c // 2, 2 * (c % 2))
                    put_chunk(dve, c // 2, 2 * (c % 2))
                    if c + 1 < C:
                        lo_of(dve, vt_hi, c + 2, vt_split[:, LO], vt_split[:, HI], halves(vt_banks[(c + 1) % 2]), vt_lo)
                    lo_of(dve, v_hi, c + 1, v_part(v0, LO, c), v_part(v0, HI, c), halves(v_bank), v_lo)
                    if c == 1:
                        lo_x(1)
                    if c == C - 1:
                        lo_of(dve, q_hi, 1, q_split[:, LO], q_split[:, HI], halves(y_bank), y_added, SCALE / 2)
                    mark_chunk(dve, c // 2, 2 * (c % 2) + 1)
                    put_chunk(dve, c // 2, 2 * (c % 2) + 1)
                nc.vector.tensor_copy(no_mask[:, TILES:TILES + 1], no_mask[:, 0:1]).then_inc(no_mask_copied, 1)
                dve.wait_ge(m_stored, 16 * 3)
                for b in range(BANKS):
                    dve.wait_ge(scores_done, b + 1)
                    score(b, 0)
                row_max(dve, BANKS, 1)

            @block.tensor
            def _(pe):
                def early_vt(c):
                    pe.wait_ge(w_lo["w_v"], c + 1)
                    if c >= 2:
                        pe.wait_ge(vt_lo, c - 1)
                    project(vt_banks[c % 2], w_split["w_v"], xt[0]).then_inc(vt_done, 1)

                pe.wait_ge(ident_ready, 1)
                turn_x(pe, 0, x_banks[0], 16)
                pe.wait_ge(xt_lo, 1)
                early_vt(0)
                for c in range(C):
                    pe.wait_ge(w_lo["w_k"], c + 1)
                    if c >= 1:
                        pe.wait_ge(k_lo, c)
                    project(k_bank, w_split["w_k"], xt[0]).then_inc(k_done, 1)
                    if c + 1 < C:
                        early_vt(c + 1)
                    if c == 0:
                        pe.wait_ge(wout_lo, 1)
                    if c == C - 1:
                        pe.wait_ge(w_lo["w_q"], 1)
                        project(y_bank, w_split["w_q"], xt[0]).then_inc(q_done, 1)
                    pe.wait_ge(vt_lo, c + 1)
                    if c >= 1:
                        pe.wait_ge(v_lo, c)
                    project(v_bank, vt_split, w_out).then_inc(v_done, 1)
                    if c == 1:
                        turn_x(pe, 1, x_banks[1], 32)
                pe.wait_ge(k_lo, C)
                pe.wait_ge(xt_lo, 2)
                pe.wait_ge(y_added, 1)
                for b in range(BANKS):
                    scores(k0, 0, b)

        k_split, v_split = [k0, k1], [v0, v1]
        bn_ready, mv_ready, ln_var, ln_std = sem("bn_ready"), sem("mv_ready"), sem("ln_var"), sem("ln_std")
        ln_step, normed, stored = sem("ln_step"), sem("normed"), sem("stored")

        BUILD_BLOCKS = (TILES - EARLY_TILES) // HALVES

        def at(eng, value):
            return value if isinstance(value, int) else eng.snap(value)

        def heads(eng, block_steps, unroll_last=False):
            def one_head(par, h, has_next, more_x):
                block_steps(par, h, 0, has_next, more_x, False)
                with eng.Fori(1, C - 1) as c:
                    block_steps(par, h, c, has_next, more_x, False)
                block_steps(par, h, C - 1, has_next, more_x, False)

            block_steps(0, 0, 0, True, True, True)
            with eng.Fori(1, BUILD_BLOCKS) as c:
                block_steps(0, 0, c, True, True, True)
            for c in range(BUILD_BLOCKS, C):
                block_steps(0, 0, c, True, True, False)
            with eng.Fori(0, (H - 3) // 2) as pair:
                for par in (1, 0):
                    one_head(par, eng.snap(pair * 2 + (2 - par)), True, True)
            one_head(1, H - 3, True, True)
            one_head(0, H - 2, True, False)
            if unroll_last:
                for c in range(C):
                    block_steps(1, H - 1, c, False, False, False)
            else:
                one_head(1, H - 1, False, False)

        def place_of(eng, h, c):
            if isinstance(h, int):
                n = h * C + c if isinstance(c, int) else eng.snap(c + h * C)
            else:
                n = eng.snap(h * C + c)
            return n, isinstance(c, int) and c == 0, isinstance(c, int) and c == C - 1


        with nc.Block() as block:
            @block.sync
            def _(sp):
                def build_loads(c, f, more_adj):
                    v = c * 2 + (EARLY_TILES + f)
                    for q in range(BANKS):
                        sp.wait_ge(m_chunk, v * BANKS + (q + 1))
                        if more_adj or f == 0:
                            load_adj(sp, q, c + (EARLY_TILES // 2 + f), 1 - f)
                    sp.wait_ge(m_stored, v * 16)
                    store_m(sp, v)

                def block_steps(par, h, c, has_next, more_x, builds, more_adj=True):
                    n, opens, closes = place_of(sp, h, c)
                    s4 = at(sp, n * 8)
                    if isinstance(h, int) and h == 0 and isinstance(c, int) and c == C - 2:
                        sp.wait_ge(m_stored, 16 * TILES)
                    for f in range(HALVES):
                        if has_next or not closes:
                            first = at(sp, s4 + (4 * f + 5))
                            for b in range(BANKS):
                                sp.wait_ge(scored, first + b)
                                load_m(sp, b, f if closes else c * 2 + (f + 2))
                        if f == 0:
                            if has_next or not (isinstance(c, int) and c >= C - 2):
                                sp.wait_ge(w_lo["w_q"], n + 2)
                                load_raw(sp, "w_q", (c + 2) % C if isinstance(c, int) else c + 2)
                            if has_next and (more_x or not closes):
                                for name in ("w_k", "w_v"):
                                    sp.wait_ge(w_lo[name], n + (C + 1))
                                    load_raw(sp, name, (c + 1) % C if isinstance(c, int) else c + 1)
                            if more_x and isinstance(c, int) and c == C - 2:
                                sp.wait_ge(q_done, n + 2)
                                load_x(sp, par, h + 2)
                        if builds:
                            build_loads(c, f, more_adj)
                    if more_x and closes:
                        sp.wait_ge(v_done, n + (C + 1))
                        load_wout(sp, h + 2)

                def one_head(par, h, has_next, more_x):
                    with sp.Fori(0, C - 2) as c:
                        block_steps(par, h, c, has_next, more_x, False)
                    for c in range(C - 2, C):
                        block_steps(par, h, c, has_next, more_x, False)

                with sp.Fori(0, BUILD_BLOCKS - 1) as c:
                    block_steps(0, 0, c, True, True, True)
                block_steps(0, 0, BUILD_BLOCKS - 1, True, True, True, more_adj=False)
                for c in range(BUILD_BLOCKS, C):
                    block_steps(0, 0, c, True, True, False)
                with sp.Fori(0, (H - 3) // 2) as pair:
                    for par in (1, 0):
                        one_head(par, sp.snap(pair * 2 + (2 - par)), True, True)
                one_head(1, H - 3, True, True)
                one_head(0, H - 2, True, False)
                one_head(1, H - 1, False, False)
                for c in range(0, C, 2):
                    sp.wait_ge(normed, HALVES * (c + 2))
                    for f in range(HALVES):
                        sp.dma_start(out_tokens[f][:, c:c + 2], y_tokens[:, f, c:c + 2]).then_inc(stored, 16)
                sp.wait_ge(stored, 16 * TILES // 2)

            @block.tensor
            def _(pe):
                def turn(g):
                    for j in range(TPB):
                        mm = nc.tensor.transpose(pt_bank[g % 2][:, j * P:(j + 1) * P],
                                                 t_p[:, (TPB * g + j) * P:(TPB * g + j + 1) * P], ident[:])
                    mm.then_inc(turned, 1)

                def values(par, g, has_next, tiles=range(TPB)):
                    for j in tiles:
                        v = v_split[par][:, TPB * g + j]
                        hi_v = (y_bank[:], pt_group(HI, g, not has_next)[:, j * P:(j + 1) * P], v.rearrange("p s d -> p (s d)"))
                        lo_v = (y_bank[:, 0:D], pt_group(LO, g, not has_next)[:, j * P:(j + 1) * P], v[:, HI])
                        if g == 0 and j == 0:
                            nc.tensor.matmul(*hi_v, start=True, stop=False)
                            mm = nc.tensor.matmul(*lo_v, start=False, stop=False)
                        else:
                            nc.tensor.matmul(*lo_v, start=False, stop=False)
                            mm = nc.tensor.matmul(*hi_v, start=False, stop=(g == BANKS - 1 and j == TPB - 1))
                    return mm

                def step(par, f, h, n, has_next, more_x, opens, closes):
                    s4 = at(pe, n * 8 + 4 * f)
                    s1 = n * 2 + f
                    has_scores = has_next or not (closes and f == 1)
                    has_q = f == 0 and (has_next or not closes)
                    for g in range(BANKS):
                        if g == 0:
                            pe.wait_ge(exp_done, s1 + 1)
                        if g == 3 and not has_next:
                            pe.wait_ge(pt_lo, s4 + 2)
                        turn(g)
                        if has_scores:
                            if g == 0 and f == 1:
                                pe.wait_ge(q_lo, n + 1)
                                if closes:
                                    pe.wait_ge(k_lo, n + (C + 1))
                            pe.wait_ge(scored, s4 + (g + 1))
                            scores(k_split[1 - par if closes and f == 1 else par], 1 - f, g)
                        if g == 1:
                            pe.wait_ge(pt_lo, s4 + 1)
                            pe.wait_ge(y_added, s1 + 1)
                            if f == 0:
                                pe.wait_ge(v_lo, n + C if has_next else H * C)
                            if f == 0 and closes and more_x:
                                turn_x(pe, par, proj_bank, h * 16 + 48)
                            values(par, 0, has_next)
                            if has_next and f == 1:
                                pe.wait_ge(w_lo["w_v"], n + (C + 1))
                                pe.wait_ge(k_lo, n + (C + 1))
                                project(proj_bank, w_split["w_v"], xt[1 - par]).then_inc(vt_done, 1)
                        if g == 2 and has_next:
                            pe.wait_ge(pt_lo, s4 + 2)
                            values(par, 1, has_next)
                        if g == 3 and not has_next:
                            values(par, 1, has_next)
                    if has_q:
                        pe.wait_ge(w_lo["w_q"], n + 2)
                        if closes and more_x:
                            pe.wait_ge(xt_lo, h + 3)
                        if not has_next:
                            pe.wait_ge(q_lo, n)
                        project(proj_bank, w_split["w_q"], xt[1 - par if closes else par]).then_inc(q_done, 1)
                    pe.wait_ge(pt_lo, s4 + 3)
                    values(par, 2, has_next)
                    if f == 0:
                        pe.wait_ge(pt_lo, s4 + 4)
                        values(par, 3, has_next, range(TPB // 2))
                    if has_next and f == 0:
                        pe.wait_ge(w_lo["w_k"], n + (C + 1))
                        pe.wait_ge(q_lo, n + 1)
                        project(proj_bank, w_split["w_k"], xt[1 - par]).then_inc(k_done, 1)
                    if has_next and f == 1:
                        pe.wait_ge(vt_lo, n + (C + 1))
                        if opens:
                            pe.wait_ge(wout_lo, h + 2)
                        project(proj_bank, vt_split, w_out).then_inc(v_done, 1)
                    if f == 1:
                        pe.wait_ge(pt_lo, s4 + 4)
                    values(par, 3, has_next, range(TPB // 2 if f == 0 else 0, TPB)).then_inc(y_done, 1)

                def block_steps(par, h, c, has_next, more_x, builds):
                    n, opens, closes = place_of(pe, h, c)
                    for f in range(HALVES):
                        step(par, f, h, n, has_next, more_x, opens, closes)

                heads(pe, block_steps)

            @block.gpsimd
            def _(pool):
                def block_steps(par, h, c, has_next, more_x, builds):
                    n, opens, closes = place_of(pool, h, c)
                    if has_next or not closes:
                        lo_w(pool, "w_q", raw["w_q"][:], n + 2)
                    if has_next:
                        lo_w(pool, "w_k", raw["w_k"][:], n + (C + 1))
                        lo_w(pool, "w_v", raw["w_v"][:], n + (C + 1))
                    if has_next and opens:
                        lo_wout(pool, h + 2)
                heads(pool, block_steps)

            @block.scalar
            def _(act):
                def block_steps(par, h, c, has_next, more_x, builds):
                    n, opens, closes = place_of(act, h, c)

                    def hi_next(name, used, uses):
                        hi_w(act, name, raw[name][:], raw_loaded[name], n * 16 + 16, used, uses)

                    for f in range(HALVES):
                        s4 = at(act, n * 8 + 4 * f)
                        for g in range(BANKS):
                            hi_of(act, turned, s4 + (g + 1), pt_group(HI, g, not has_next), pt_bank[g % 2][:], pt_hi)
                            if f == 0:
                                if g == 0 and (has_next or not closes):
                                    hi_next("w_q", q_done, n + 1)
                                if g == 1 and has_next:
                                    hi_next("w_k", k_done, n + C)
                                if g == 2 and has_next:
                                    hi_next("w_v", vt_done, n + C)
                                if g == 1 and closes and more_x:
                                    hi_of(act, xt_turned, h + 3, xt[par][:, HI], halves(proj_bank), xt_hi)
                                if g == 3 and opens and has_next:
                                    hi_wout(act, h + 2)
                            if g == 1 and f == 1 and has_next:
                                hi_of(act, vt_done, n + (C + 1), vt_split[:, HI], halves(proj_bank), vt_hi)
                        if f == 0 and (has_next or not closes):
                            hi_of(act, q_done, n + 2, q_split[:, HI], halves(proj_bank), q_hi, SCALE / 2)
                        if has_next or not (closes and f == 1):
                            exp_tile(act, n * 2 + (f + 2))
                        if has_next and f == 0:
                            hi_of(act, k_done, n + (C + 1), k_part(k_split[1 - par], HI, c), halves(proj_bank), k_hi)
                        if has_next and f == 1:
                            hi_of(act, v_done, n + (C + 1), v_part(v_split[1 - par], HI, c), halves(proj_bank), v_hi)
                heads(act, block_steps)

                act.wait_ge(ln_var, 1)
                nc.scalar.activation(std, var_eps, ACT.Sqrt).then_inc(ln_std, 1)

            @block.vector
            def _(dve):
                def step(par, f, h, n, c, has_next, more_x, builds, opens, closes):
                    s4 = at(dve, n * 8 + 4 * f)
                    s1 = at(dve, n * 2 + f)
                    has_scores = has_next or not (closes and f == 1)
                    v = at(dve, c * HALVES + (f + EARLY_TILES)) if builds else None
                    ends_build = isinstance(h, int) and h == 0 and (
                        not opens or f == 1 if builds else c == BUILD_BLOCKS and f == 0)
                    last_v = at(dve, c * HALVES + (f + EARLY_TILES - 1)) if ends_build else None
                    for g in range(BANKS):
                        if has_scores:
                            dve.wait_ge(scores_done, s4 + (5 + g))
                            dve.wait_ge(m_loaded[g], s1 * 16 + 16)
                        lo_of(dve, pt_hi, s4 + (g + 1), pt_group(LO, g, not has_next), pt_group(HI, g, not has_next),
                              pt_bank[g % 2][:], pt_lo)
                        if has_scores:
                            score(g, c * HALVES + (f + 1))
                        if g == 0:
                            dve.wait_ge(exp_done, s1 + 1)
                            dve.wait_ge(floor_done, s1 + 1)
                            nc.vector.scalar_tensor_tensor(out=denom, in0=floor_exp,
                                                           scalar=count[:, bass.ds(c * HALVES + f, 1)], in1=row_sum,
                                                           op0=ALU.mult, op1=ALU.add).then_inc(denom_ready, 1)
                            dve.wait_ge(denom_ready, s1 + 1)
                            nc.vector.reciprocal(rdenom, denom).then_inc(rdenom_ready, 1)
                        if g == 0 and ends_build:
                            put_chunk(dve, last_v, BANKS - 1)
                        if g == 1 and builds:
                            mark_chunk(dve, v, 0)
                        if g == 1 and f == 0 and closes and more_x:
                            lo_of(dve, xt_hi, h + 3, xt[par][:, LO], xt[par][:, HI], halves(proj_bank), xt_lo)
                        if g == 1 and f == 1 and has_next:
                            lo_of(dve, vt_hi, n + (C + 1), vt_split[:, LO], vt_split[:, HI],
                                  halves(proj_bank), vt_lo)
                    if has_scores:
                        row_max(dve, s4 + 8, s1 + 2)
                    if f == 0 and (has_next or not closes):
                        lo_of(dve, q_hi, n + 2, q_split[:, LO], q_split[:, HI], halves(proj_bank), q_lo, SCALE / 2)
                    if builds:
                        for q in range(BANKS - 1):
                            if q:
                                mark_chunk(dve, v, q)
                            put_chunk(dve, v, q)
                    if has_next and f == 0:
                        lo_of(dve, k_hi, n + (C + 1), k_part(k_split[1 - par], LO, c), k_part(k_split[1 - par], HI, c),
                              halves(proj_bank), k_lo)
                    if has_next and f == 1:
                        lo_of(dve, v_hi, n + (C + 1), v_part(v_split[1 - par], LO, c), v_part(v_split[1 - par], HI, c),
                              halves(proj_bank), v_lo)
                    if builds:
                        mark_chunk(dve, v, 3)
                    tile = c * HALVES + f
                    y = y_acc[:, tile, :] if isinstance(tile, int) else \
                        y_acc[:, bass.ds(tile, 1), :].rearrange("p a d -> p (a d)")
                    if isinstance(h, int) and h == 0 and opens:
                        dve.wait_ge(y_init, 32)
                    dve.wait_ge(y_done, s1 + 1)
                    dve.wait_ge(rdenom_ready, s1 + 1)
                    nc.vector.scalar_tensor_tensor(out=y, in0=y_bank[:, 0:D], scalar=rdenom, in1=y,
                                                   op0=ALU.mult, op1=ALU.add).then_inc(y_half, 1)
                    dve.wait_ge(y_half, s1 + 1)
                    nc.vector.scalar_tensor_tensor(out=y, in0=y_bank[:, D:2 * D], scalar=rdenom, in1=y,
                                                   op0=ALU.mult, op1=ALU.add).then_inc(y_added, 1)
                    if not has_next:
                        dve.wait_ge(y_added, s1 + 2)
                        nc.vector.bn_stats(bn, y).then_inc(bn_ready, 1)
                        tile = c * HALVES + f
                        dve.wait_ge(bn_ready, tile + 1)
                        nc.vector.bn_aggr(mean_var[:, tile, :], bn).then_inc(mv_ready, 1)

                def block_steps(par, h, c, has_next, more_x, builds):
                    n, opens, closes = place_of(dve, h, c)
                    for f in range(HALVES):
                        step(par, f, h, n, c, has_next, more_x, builds, opens, closes)
                heads(dve, block_steps, unroll_last=True)

                dve.wait_ge(mv_ready, TILES)
                nc.vector.tensor_scalar(var_eps, mean_var[:, :, 1], EPS, None, ALU.add).then_inc(ln_var, 1)
                dve.wait_ge(ln_std, 1)
                nc.vector.reciprocal(rstd, std).then_inc(ln_step, 1)
                dve.wait_ge(ln_step, 1)
                nc.vector.tensor_tensor(newton, rstd, rstd, ALU.mult).then_inc(ln_step, 1)
                dve.wait_ge(ln_step, 2)
                nc.vector.tensor_tensor(std, newton, var_eps, ALU.mult).then_inc(ln_step, 1)
                dve.wait_ge(ln_step, 3)
                nc.vector.tensor_scalar(newton, std, -0.5, 1.5, ALU.mult, ALU.add).then_inc(ln_step, 1)
                dve.wait_ge(ln_step, 4)
                nc.vector.tensor_tensor(var_eps, newton, rstd, ALU.mult).then_inc(ln_step, 1)
                dve.wait_ge(ln_step, 5)
                inv = var_eps
                for t in range(TILES):
                    nc.vector.tensor_scalar(y_acc[:, t, :], y_acc[:, t, :], mean_var[:, t, 0:1], inv[:, t:t + 1],
                                            ALU.subtract, ALU.mult).then_inc(normed, 1)


_INS = ["x", "adj", "L0_gnn_Wq", "L0_gnn_Wk", "L0_gnn_Wv", "L0_gnn_Wout"]


def kernel(**inputs):
    import numpy as _np
    import concourse.bacc as _bacc
    from concourse.bass_utils import run_bass_kernel_spmd as _run

    nc = _bacc.Bacc("TRN2", target_bir_lowering=False, num_devices=1)
    arrays, args = {}, []
    for name in _INS:
        a = _np.ascontiguousarray(inputs[name])
        arrays[f"in_{name}_dram"] = a
        args.append(nc.dram_tensor(f"in_{name}_dram", a.shape, mybir.dt.from_np(a.dtype), kind="ExternalInput").ap())
    args.append(nc.dram_tensor("out_0_dram", inputs["x"].shape, F32, kind="ExternalOutput").ap())
    graph_attention_layernorm(nc, *args)
    r = _run(nc, [arrays], core_ids=[0])
    return r.results[0]["out_0_dram"]
```

```python
from contextlib import ExitStack

import concourse.bass as bass
from concourse import mybir

F32 = mybir.dt.float32
F32R = mybir.dt.float32r
ALU = mybir.AluOpType
ACT = mybir.ActivationFunctionType
AX_X = mybir.AxisListType.X

P = 128
BANK = 512
HI, LO = 0, 1
BIG = 2.0 ** 100
FLOOR = -1.0e6
NO_FLOOR = -(2.0 ** 120)
LOWEST = -3.0e38
EPS = 1e-5


def columns(w, c, size):
    return w.rearrange("(k p) n -> p k n", p=P)[:, :, bass.ds(c * size, size)]


def graph_attention_layernorm(nc, x, adj, wq, wk, wv, wout, out):
    N, D = x.shape
    H = wq.shape[1] // D
    C = N // (N // H)
    R = N // H
    KC = D // P
    HALVES = R // P
    TILES = C * HALVES
    BANKS = N // BANK
    TPB = BANK // P
    SCALE = float(D) ** -0.5
    assert C == H and KC == 2 and HALVES == 2 and BANKS == 4 and BANK == KC * R

    with ExitStack() as ctx:
        def sem(name):
            return ctx.enter_context(nc.semaphore(name))

        def sbuf(name, shape, dt=F32, where=ctx):
            return where.enter_context(nc.sbuf_tensor(name, shape, dt))

        m_dram = nc.dram_tensor("m_dram", [TILES, P, N], F32, kind="Internal").ap()

        y_acc = sbuf("y_acc", [P, TILES, D])
        ident = sbuf("ident", [P, P])
        k0 = sbuf("k0", [P, 2, KC, N], F32R)
        v0 = sbuf("v0", [P, TILES, 2, D], F32R)
        q_split = sbuf("q_split", [P, 2, KC, R], F32R)
        vt_split = sbuf("vt_split", [P, 2, KC, R], F32R)
        w_split = {n: sbuf(n, [P, 2, KC, D], F32R) for n in ("w_q", "w_k", "w_v")}
        before = ExitStack()
        low_places = []
        for what in ("x0", "x1", "wout"):
            sbuf("high_of_" + what, [P, KC, D], where=before)
            low_places.append(sbuf("raw_" + what, [P, KC, D], where=before))
        raw_x, raw_wout = low_places[:2], low_places[2]
        before.close()
        xt = [sbuf(f"xt{par}", [P, 2, KC, D], F32R) for par in range(2)]
        w_out = sbuf("w_out", [P, 2, KC, D], F32R)
        raw = {n: sbuf("raw_" + n, [P, KC, D]) for n in ("w_q", "w_k", "w_v")}
        m_sb = sbuf("m_sb", [P, BANKS, BANK])
        t_p = sbuf("t_p", [P, N])
        zero_mark = sbuf("zero_mark", [P, BANK], mybir.dt.uint8)
        small = sbuf("small", [P, 160])

        taken = [0]

        def part_of_small(n):
            taken[0] += n
            return small[:, taken[0] - n:taken[0]]

        bank_max = part_of_small(BANKS + 1)
        neg_max, row_sum, floor_exp, denom, rdenom = (part_of_small(1) for _ in range(5))
        chunk_count = part_of_small(BANKS)
        count = part_of_small(TILES)
        no_mask = part_of_small(TILES + 1)
        bn = part_of_small(6)
        mean_var = part_of_small(2 * TILES).rearrange("p (t s) -> p t s", s=2)
        var_eps, std, rstd, newton, inv = (m_sb[:, 0, i * TILES:(i + 1) * TILES] for i in range(5))

        bank = [ctx.enter_context(nc.psum_tensor(f"bank{b}", [P, BANK], F32)) for b in range(8)]
        score_bank, pt_bank, y_bank, proj_bank = bank[0:4], bank[4:6], bank[6], bank[7]

        x_loaded, xt_turned, xt_hi, xt_lo = sem("x_loaded"), sem("xt_turned"), sem("xt_hi"), sem("xt_lo")
        wout_loaded, wout_hi, wout_lo = sem("wout_loaded"), sem("wout_hi"), sem("wout_lo")
        y_init = sem("y_init")
        m_loaded = [sem(f"m_loaded{b}") for b in range(BANKS)]
        q_done, k_done, vt_done, v_done = sem("q_done"), sem("k_done"), sem("vt_done"), sem("v_done")
        q_hi, k_hi, vt_hi, v_hi = sem("q_hi"), sem("k_hi"), sem("vt_hi"), sem("v_hi")
        q_lo, k_lo, vt_lo, v_lo = sem("q_lo"), sem("k_lo"), sem("vt_lo"), sem("v_lo")
        scores_done, scored = sem("scores_done"), sem("scored")
        w_hi = {n: sem("hi_" + n) for n in raw}
        w_lo = {n: sem("lo_" + n) for n in raw}
        raw_loaded = {n: sem("loaded_raw_" + n) for n in raw}
        adj_loaded = [sem(f"adj_loaded{i}") for i in range(BANKS)]
        marked, m_chunk, counted, m_stored = sem("marked"), sem("m_chunk"), sem("counted"), sem("m_stored")
        floor_copied, max_ready, exp_done, floor_done = (sem("floor_copied"), sem("max_ready"), sem("exp_done"),
                                                         sem("floor_done"))
        denom_ready, rdenom_ready = sem("denom_ready"), sem("rdenom_ready")
        floors_ready = sem("floors_ready")
        turned, pt_hi, pt_lo = sem("turned"), sem("pt_hi"), sem("pt_lo")
        y_done, y_half, y_added = sem("y_done"), sem("y_half"), sem("y_added")

        adj_rows = adj.rearrange("(f p c) j -> c f p j", f=HALVES, c=C)
        x_tokens = x.rearrange("(f p c) e -> f p c e", f=HALVES, c=C)
        out_tokens = out.rearrange("(f p c) e -> f p c e", f=HALVES, c=C)
        y_tokens = y_acc[:].rearrange("p (c f) e -> p f c e", f=HALVES)

        TERMS = [(a, b, k) for k in range(KC) for a, b in ((HI, HI), (HI, LO), (LO, HI))]

        def project(dst, left, right):
            for o in range(2):
                for i, (a, b, k) in enumerate(TERMS):
                    mm = nc.tensor.matmul(dst[:, o * R:(o + 1) * R], left[:, a, k, o * P:(o + 1) * P],
                                          right[:, b, k, :], start=(i == 0), stop=(i == len(TERMS) - 1))
            return mm

        def scores(k_both, f, b):
            for i, (a, kk, k) in enumerate(TERMS):
                mm = nc.tensor.matmul(score_bank[b][:], q_split[:, a, k, f * P:(f + 1) * P],
                                      k_both[:, kk, k, b * BANK:(b + 1) * BANK],
                                      start=(i == 0), stop=(i == len(TERMS) - 1))
            mm.then_inc(scores_done, 1)

        def turn_x(pe, par, bank_of_x, loads):
            pe.wait_ge(x_loaded, loads)
            for kc in range(KC):
                for f in range(HALVES):
                    mm = nc.tensor.transpose(bank_of_x[:, kc * R + f * P:kc * R + (f + 1) * P],
                                             raw_x[par][:, f, kc * P:(kc + 1) * P], ident[:])
            mm.then_inc(xt_turned, 1)

        def hi_of(act, done, value, dst, src, hi_sem, scale=1.0):
            act.wait_ge(done, value)
            nc.scalar.activation(dst, src, ACT.Copy, scale=scale).then_inc(hi_sem, 1)

        def exp_tile(act, value):
            act.wait_ge(max_ready, value)
            nc.scalar.activation(t_p[:], t_p[:], ACT.Exp, bias=neg_max, scale=1.0,
                                 accum_out=row_sum).then_inc(exp_done, 1)
            nc.scalar.activation(floor_exp, bank_max[:, BANKS:BANKS + 1], ACT.Exp, bias=neg_max,
                                 scale=1.0).then_inc(floor_done, 1)

        def hi_w(act, name, src, loads_sem, loads, used, uses):
            act.wait_ge(loads_sem, loads)
            if uses is not None:
                act.wait_ge(used, uses)
            nc.scalar.activation(w_split[name][:, HI], src, ACT.Copy).then_inc(w_hi[name], 1)

        def hi_wout(act, pieces):
            act.wait_ge(wout_loaded, pieces * 16)
            nc.scalar.activation(w_out[:, HI], raw_wout[:], ACT.Copy).then_inc(wout_hi, 1)

        def lo_w(eng, name, src, value):
            eng.wait_ge(w_hi[name], value)
            eng.tensor_tensor(w_split[name][:, LO], src, w_split[name][:, HI].bitcast(F32),
                              ALU.subtract).then_inc(w_lo[name], 1)

        def lo_wout(pool, value):
            pool.wait_ge(wout_hi, value)
            nc.gpsimd.tensor_tensor(w_out[:, LO], raw_wout[:], w_out[:, HI].bitcast(F32),
                                    ALU.subtract).then_inc(wout_lo, 1)

        def lo_of(dve, hi_sem, value, dst, hi, src, lo_sem, scale=None):
            dve.wait_ge(hi_sem, value)
            if scale is None:
                ins = nc.vector.tensor_tensor(dst, src, hi.bitcast(F32), ALU.subtract)
            else:
                ins = nc.vector.scalar_tensor_tensor(out=dst, in0=src, scalar=scale, in1=hi.bitcast(F32),
                                                     op0=ALU.mult, op1=ALU.subtract)
            ins.then_inc(lo_sem, 1)

        def score(b, tile):
            if b == 0:
                nc.vector.tensor_scalar(bank_max[:, BANKS:BANKS + 1], no_mask[:, bass.ds(tile, 1)], FLOOR, None,
                                        ALU.add).then_inc(floor_copied, 1)
            nc.vector.tensor_tensor_reduce(out=t_p[:, b * BANK:(b + 1) * BANK], in0=score_bank[b][:],
                                           in1=m_sb[:, b, :], scale=2.0, scalar=LOWEST, op0=ALU.add,
                                           op1=ALU.max, accum_out=bank_max[:, b:b + 1]).then_inc(scored, 1)

        def row_max(dve, value, floors):
            dve.wait_ge(floor_copied, floors)
            dve.wait_ge(scored, value)
            nc.vector.tensor_reduce(neg_max, bank_max, AX_X, ALU.max, negate=True).then_inc(max_ready, 1)

        def m_made(v):
            first = {0: m_sb[:].rearrange("p b k -> p (b k)"), 2: t_p[:]}
            return first.get(v, m_build[:]) if isinstance(v, int) else m_build[:]

        def mark_chunk(dve, v, q):
            s4 = v * BANKS if isinstance(v, int) else dve.snap(v * BANKS)
            dve.wait_ge(adj_loaded[q], v * 16 + 16)
            if not (isinstance(v, int) and v == 0 and q == 0):
                dve.wait_ge(m_chunk, s4 + q if q else s4)
            nc.vector.tensor_scalar(zero_mark[:], adj_chunk[q][:], 0.0, None, ALU.is_equal, ALU.add,
                                    accum_out=chunk_count[:, q:q + 1]).then_inc(marked, 1)

        def put_chunk(dve, v, q):
            rows = BANK // C
            s4 = v * BANKS if isinstance(v, int) else dve.snap(v * BANKS)
            dve.wait_ge(marked, s4 + (q + 1))
            if q == 0 and isinstance(v, int) and v == 3:
                dve.wait_ge(m_stored, 16 * 2)
            if q == 0 and not (isinstance(v, int) and v <= 3):
                dve.wait_ge(m_stored, v * 16)
            nc.vector.scalar_tensor_tensor(
                out=m_made(v).rearrange("p (c r) -> p c r", c=C)[:, :, q * rows:(q + 1) * rows],
                in0=zero_mark[:].rearrange("p (r c) -> p c r", c=C), scalar=-BIG,
                in1=adj_chunk[q][:].rearrange("p (r c) -> p c r", c=C),
                op0=ALU.mult, op1=ALU.add).then_inc(m_chunk, 1)
            if q == BANKS - 1:
                nc.vector.tensor_reduce(count[:, bass.ds(v, 1)], chunk_count, AX_X, ALU.add).then_inc(counted, 1)
                dve.wait_ge(counted, v + 1)
                nc.vector.tensor_scalar(no_mask[:, bass.ds(v, 1)], count[:, bass.ds(v, 1)], 0.0, NO_FLOOR,
                                        ALU.is_equal, ALU.mult).then_inc(floors_ready, 1)

        def build_chunk(dve, v, q):
            mark_chunk(dve, v, q)
            put_chunk(dve, v, q)

        def k_part(k_both, part, c):
            return k_both[:, part, :, bass.ds(c * R, R)]

        def v_part(v_both, part, c):
            return v_both[:, bass.ds(c * HALVES, HALVES), part, :]

        def halves(bank_ap):
            return bank_ap[:].rearrange("p (o r) -> p o r", o=2)

        def rows_of(w, h):
            return w[bass.ds(h * R, R), :].rearrange("(a p) e -> p a e", p=P)

        def load_x(sp, par, h):
            sp.dma_start(raw_x[par][:], rows_of(x, h)).then_inc(x_loaded, 16)

        def load_wout(sp, h):
            sp.dma_start(raw_wout[:], rows_of(wout, h)).then_inc(wout_loaded, 16)

        def load_raw(sp, name, c):
            w = {"w_q": wq, "w_k": wk, "w_v": wv}[name]
            sp.dma_start(raw[name][:], columns(w, c, D)).then_inc(raw_loaded[name], 16)

        def load_adj(sp, q, c, f):
            sp.dma_start(adj_chunk[q][:], adj_rows[c, f][:, q * BANK:(q + 1) * BANK]).then_inc(adj_loaded[q], 16)

        def store_m(sp, tile):
            sp.dma_start(m_dram[tile], m_made(tile)).then_inc(m_stored, 16)

        def load_m(sp, b, tile):
            sp.dma_start(m_sb[:, b, :], m_dram[tile][:, b * BANK:(b + 1) * BANK]).then_inc(m_loaded[b], 16)

        early = ExitStack()
        places, adj_chunk = [], []

        def place():
            places.append(sbuf(f"place{len(places)}", [P, KC, D], where=early))

        for row in range(2 * KC):
            for _ in range(N // BANK - 1):
                place()
            adj_chunk.append(sbuf(f"adj_chunk{row}", [P, BANK], where=early))
        for _ in range(TILES - BANKS):
            place()
        m_build = sbuf("m_build", [P, N], where=early)
        early.close()
        k1 = sbuf("k1", [P, 2, KC, N], F32R)
        v1 = sbuf("v1", [P, TILES, 2, D], F32R)
        PT_SLOTS = 2
        pt = [sbuf(f"pt_{'hl'[part]}", [P, PT_SLOTS, BANK], F32R) for part in (HI, LO)]

        def pt_group(part, g, last_head):
            if last_head and g == BANKS - 1:
                return k0[:, part, 0, 0:BANK]
            return pt[part][:, g % PT_SLOTS, :]

        EARLY_TILES = 4

        early_w = {("w_v", c): places[2 * c] for c in range(C)}
        early_w.update({("w_k", c): places[2 * c + 1] for c in range(C)})
        early_w["w_q", 0] = places[2 * C]
        early_loaded = {key: sem("loaded_early_%s%d" % key) for key in early_w}
        ident_ready, ident_filled, no_mask_copied = sem("ident_ready"), sem("ident_filled"), sem("no_mask_copied")
        w_src = {"w_k": wk, "w_q": wq, "w_v": wv}
        Q_ROUND = 4
        chunks = [(t, q) for t in range(EARLY_TILES) for q in range(BANKS)]
        LATE_CHUNKS = 2
        k_bank, vt_banks, x_banks, v_bank = score_bank[0], pt_bank, score_bank[1:3], proj_bank

        def after_chunk(sp, t, q):
            sp.wait_ge(m_chunk, t * BANKS + q + 1)
            if q == BANKS - 1:
                if t:
                    sp.wait_ge(m_stored, 16 * t)
                store_m(sp, t)
            load_adj(sp, q, (t + 1) // 2, (t + 1) % 2)

        with nc.Block() as block:
            @block.sync
            def _(sp):
                def load_early(name, c):
                    sp.dma_start(early_w[name, c][:], columns(w_src[name], c, D)).then_inc(early_loaded[name, c], 16)

                load_x(sp, 0, 0)
                load_early("w_v", 0)
                load_early("w_k", 0)
                load_wout(sp, 0)
                load_early("w_v", 1)
                for q in range(BANKS // 2):
                    load_adj(sp, q, 0, 0)
                load_early("w_k", 1)
                sp.wait_ge(x_loaded, 16)
                load_x(sp, 1, 1)
                for q in range(BANKS // 2, BANKS):
                    load_adj(sp, q, 0, 0)
                for c in range(2, C):
                    load_early("w_v", c)
                    load_early("w_k", c)
                    if c == Q_ROUND:
                        load_early("w_q", 0)
                load_raw(sp, "w_q", 1)
                load_raw(sp, "w_k", 0)
                load_raw(sp, "w_v", 0)
                for t, q in chunks[:-LATE_CHUNKS]:
                    after_chunk(sp, t, q)
                sp.wait_ge(v_done, C)
                load_wout(sp, 1)
                sp.wait_ge(m_stored, 16 * 2)
                for b in range(BANKS):
                    sp.wait_ge(scored, b + 1)
                    load_m(sp, b, 1)

            @block.gpsimd
            def _(pool):
                nc.gpsimd.memset(t_p[:, 0:P], 1.0).then_inc(ident_filled, 1)
                pool.wait_ge(ident_filled, 1)
                nc.gpsimd.affine_select(out=ident[:], in_=t_p[:, 0:P], compare_op=ALU.is_equal, fill=0.0, base=0,
                                        pattern=[[-1, P]], channel_multiplier=1).then_inc(ident_ready, 1)
                lo_w(pool, "w_k", early_w["w_k", 0][:], 1)
                lo_w(pool, "w_v", early_w["w_v", 1][:], 2)
                lo_wout(pool, 1)
                for c in range(1, C):
                    lo_w(pool, "w_k", early_w["w_k", c][:], c + 1)
                    if c + 1 < C:
                        lo_w(pool, "w_v", early_w["w_v", c + 1][:], c + 2)
                    if c == Q_ROUND - 1:
                        lo_w(pool, "w_q", early_w["w_q", 0][:], 1)

            @block.scalar
            def _(act):
                def hi_early(name, c, used):
                    hi_w(act, name, early_w[name, c][:], early_loaded[name, c], 16, used, c if c else None)

                def hi_x(c):
                    hi_of(act, xt_turned, c + 1, xt[c][:, HI], halves(x_banks[c]), xt_hi)

                hi_x(0)
                hi_early("w_v", 0, vt_done)
                hi_early("w_k", 0, k_done)
                hi_early("w_v", 1, vt_done)
                hi_of(act, vt_done, 1, vt_split[:, HI], halves(vt_banks[0]), vt_hi)
                hi_wout(act, 1)
                for c in range(C):
                    hi_of(act, k_done, c + 1, k_part(k0, HI, c), halves(k_bank), k_hi)
                    if c + 1 < C:
                        hi_early("w_k", c + 1, k_done)
                    if c + 2 < C:
                        hi_early("w_v", c + 2, vt_done)
                    act.wait_ge(v_done, c + 1)
                    if c + 1 < C:
                        hi_of(act, vt_done, c + 2, vt_split[:, HI], halves(vt_banks[(c + 1) % 2]), vt_hi)
                    hi_of(act, v_done, c + 1, v_part(v0, HI, c), halves(v_bank), v_hi)
                    if c == 1:
                        hi_x(1)
                    if c == Q_ROUND - 2:
                        hi_early("w_q", 0, q_done)
                    if c == Q_ROUND:
                        hi_of(act, q_done, 1, q_split[:, HI], halves(y_bank), q_hi, SCALE / 2)

            @block.vector
            def _(dve):
                def lo_x(c):
                    lo_of(dve, xt_hi, c + 1, xt[c][:, LO], xt[c][:, HI], halves(x_banks[c]), xt_lo)

                lo_x(0)
                lo_w(dve, "w_v", early_w["w_v", 0][:], 1)
                lo_of(dve, vt_hi, 1, vt_split[:, LO], vt_split[:, HI], halves(vt_banks[0]), vt_lo)
                for c in range(C):
                    lo_of(dve, k_hi, c + 1, k_part(k0, LO, c), k_part(k0, HI, c), halves(k_bank), k_lo)
                    if c < C - 1:
                        build_chunk(dve, c // 2, 2 * (c % 2))
                    if c + 1 < C:
                        lo_of(dve, vt_hi, c + 2, vt_split[:, LO], vt_split[:, HI], halves(vt_banks[(c + 1) % 2]), vt_lo)
                    lo_of(dve, v_hi, c + 1, v_part(v0, LO, c), v_part(v0, HI, c), halves(v_bank), v_lo)
                    if c == 1:
                        lo_x(1)
                    if c == Q_ROUND:
                        lo_of(dve, q_hi, 1, q_split[:, LO], q_split[:, HI], halves(y_bank), y_added, SCALE / 2)
                    if c < C - 1:
                        build_chunk(dve, c // 2, 2 * (c % 2) + 1)
                nc.vector.tensor_copy(no_mask[:, TILES:TILES + 1], no_mask[:, 0:1]).then_inc(no_mask_copied, 1)
                dve.wait_ge(m_stored, 16 * 3)
                for b in range(BANKS):
                    dve.wait_ge(scores_done, b + 1)
                    score(b, 0)
                row_max(dve, BANKS, 1)

            @block.tensor
            def _(pe):
                def early_vt(c):
                    pe.wait_ge(w_lo["w_v"], c + 1)
                    if c >= 2:
                        pe.wait_ge(vt_lo, c - 1)
                    project(vt_banks[c % 2], w_split["w_v"], xt[0]).then_inc(vt_done, 1)

                pe.wait_ge(ident_ready, 1)
                turn_x(pe, 0, x_banks[0], 16)
                pe.wait_ge(xt_lo, 1)
                early_vt(0)
                for c in range(C):
                    pe.wait_ge(w_lo["w_k"], c + 1)
                    if c >= 1:
                        pe.wait_ge(k_lo, c)
                    project(k_bank, w_split["w_k"], xt[0]).then_inc(k_done, 1)
                    if c + 1 < C:
                        early_vt(c + 1)
                    if c == 0:
                        pe.wait_ge(wout_lo, 1)
                    if c == Q_ROUND:
                        pe.wait_ge(w_lo["w_q"], 1)
                        project(y_bank, w_split["w_q"], xt[0]).then_inc(q_done, 1)
                    pe.wait_ge(vt_lo, c + 1)
                    if c >= 1:
                        pe.wait_ge(v_lo, c)
                    project(v_bank, vt_split, w_out).then_inc(v_done, 1)
                    if c == 1:
                        turn_x(pe, 1, x_banks[1], 32)
                pe.wait_ge(k_lo, C)
                pe.wait_ge(xt_lo, 2)
                pe.wait_ge(y_added, 1)
                for b in range(BANKS):
                    scores(k0, 0, b)

        k_split, v_split = [k0, k1], [v0, v1]
        bn_ready, mv_ready, ln_var, ln_std = sem("bn_ready"), sem("mv_ready"), sem("ln_var"), sem("ln_std")
        ln_step, normed, stored = sem("ln_step"), sem("normed"), sem("stored")

        normed_by_pool = sem("normed_by_pool")
        NORM_FIRST, NORM_LAST = 6, 8

        def normalise_tile(engine, t):
            return engine.tensor_scalar(y_acc[:, t, :], y_acc[:, t, :], mean_var[:, t, 0:1], inv[:, t:t + 1],
                                        ALU.subtract, ALU.mult)

        BUILD_BLOCKS = (TILES - EARLY_TILES) // HALVES

        def at(eng, value):
            return value if isinstance(value, int) else eng.snap(value)

        def heads(eng, block_steps, unroll_last=False):
            def one_head(par, h, has_next, more_x):
                block_steps(par, h, 0, has_next, more_x, False)
                with eng.Fori(1, C - 1) as c:
                    block_steps(par, h, c, has_next, more_x, False)
                block_steps(par, h, C - 1, has_next, more_x, False)

            block_steps(0, 0, 0, True, True, True)
            with eng.Fori(1, BUILD_BLOCKS) as c:
                block_steps(0, 0, c, True, True, True)
            for c in range(BUILD_BLOCKS, C):
                block_steps(0, 0, c, True, True, False)
            with eng.Fori(0, (H - 3) // 2) as pair:
                for par in (1, 0):
                    one_head(par, eng.snap(pair * 2 + (2 - par)), True, True)
            one_head(1, H - 3, True, True)
            one_head(0, H - 2, True, False)
            if unroll_last:
                for c in range(C):
                    block_steps(1, H - 1, c, False, False, False)
            else:
                one_head(1, H - 1, False, False)

        def place_of(eng, h, c):
            if isinstance(h, int):
                n = h * C + c if isinstance(c, int) else eng.snap(c + h * C)
            else:
                n = eng.snap(h * C + c)
            return n, isinstance(c, int) and c == 0, isinstance(c, int) and c == C - 1


        with nc.Block() as block:
            @block.sync
            def _(sp):
                for t, q in chunks[-LATE_CHUNKS:]:
                    after_chunk(sp, t, q)
                for f in range(HALVES):
                    sp.dma_start(y_tokens[:, f], x_tokens[f]).then_inc(y_init, 16)

                def build_loads(c, f, more_adj):
                    v = c * 2 + (EARLY_TILES + f)
                    for q in range(BANKS):
                        sp.wait_ge(m_chunk, v * BANKS + (q + 1))
                        if more_adj or f == 0:
                            load_adj(sp, q, c + (EARLY_TILES // 2 + f), 1 - f)
                    sp.wait_ge(m_stored, v * 16)
                    store_m(sp, v)

                def block_steps(par, h, c, has_next, more_x, builds, more_adj=True):
                    n, opens, closes = place_of(sp, h, c)
                    s4 = at(sp, n * 8)
                    if isinstance(h, int) and h == 0 and isinstance(c, int) and c == C - 2:
                        sp.wait_ge(m_stored, 16 * TILES)
                    for f in range(HALVES):
                        if has_next or not closes:
                            first = at(sp, s4 + (4 * f + 5))
                            for b in range(BANKS):
                                sp.wait_ge(scored, first + b)
                                load_m(sp, b, f if closes else c * 2 + (f + 2))
                        if f == 0:
                            if has_next or not (isinstance(c, int) and c >= C - 2):
                                sp.wait_ge(w_lo["w_q"], n + 2)
                                load_raw(sp, "w_q", (c + 2) % C if isinstance(c, int) else c + 2)
                            if has_next and (more_x or not closes):
                                for name in ("w_k", "w_v"):
                                    sp.wait_ge(w_lo[name], n + (C + 1))
                                    load_raw(sp, name, (c + 1) % C if isinstance(c, int) else c + 1)
                            if more_x and isinstance(c, int) and c == C - 2:
                                sp.wait_ge(q_done, n + 2)
                                load_x(sp, par, h + 2)
                        if builds:
                            build_loads(c, f, more_adj)
                    if more_x and closes:
                        sp.wait_ge(v_done, n + (C + 1))
                        load_wout(sp, h + 2)

                def one_head(par, h, has_next, more_x):
                    with sp.Fori(0, C - 2) as c:
                        block_steps(par, h, c, has_next, more_x, False)
                    for c in range(C - 2, C):
                        block_steps(par, h, c, has_next, more_x, False)

                with sp.Fori(0, BUILD_BLOCKS - 1) as c:
                    block_steps(0, 0, c, True, True, True)
                block_steps(0, 0, BUILD_BLOCKS - 1, True, True, True, more_adj=False)
                for c in range(BUILD_BLOCKS, C):
                    block_steps(0, 0, c, True, True, False)
                with sp.Fori(0, (H - 3) // 2) as pair:
                    for par in (1, 0):
                        one_head(par, sp.snap(pair * 2 + (2 - par)), True, True)
                one_head(1, H - 3, True, True)
                one_head(0, H - 2, True, False)
                one_head(1, H - 1, False, False)

                def store_out(first, stop):
                    for f in range(HALVES):
                        sp.dma_start(out_tokens[f][:, first:stop], y_tokens[:, f, first:stop]).then_inc(stored, 16)

                sp.wait_ge(normed, NORM_FIRST)
                store_out(0, NORM_FIRST // HALVES)
                sp.wait_ge(normed_by_pool, NORM_LAST - NORM_FIRST)
                store_out(NORM_FIRST // HALVES, NORM_LAST // HALVES)
                sp.wait_ge(normed, NORM_FIRST + 4)
                store_out(NORM_LAST // HALVES, C - 2)
                sp.wait_ge(normed, NORM_FIRST + C * HALVES - NORM_LAST - HALVES)
                store_out(C - 2, C - 1)
                for f in range(HALVES):
                    sp.wait_ge(normed, NORM_FIRST + C * HALVES - NORM_LAST - 1 + f)
                    sp.dma_start(out_tokens[f][:, C - 1], y_tokens[:, f, C - 1]).then_inc(stored, 16)
                sp.wait_ge(stored, 16 * 5 * HALVES)

            @block.tensor
            def _(pe):
                def turn(g):
                    for j in range(TPB):
                        mm = nc.tensor.transpose(pt_bank[g % 2][:, j * P:(j + 1) * P],
                                                 t_p[:, (TPB * g + j) * P:(TPB * g + j + 1) * P], ident[:])
                    mm.then_inc(turned, 1)

                def values(par, g, has_next, tiles=range(TPB)):
                    for j in tiles:
                        v = v_split[par][:, TPB * g + j]
                        p_hi, p_lo = (pt_group(part, g, not has_next)[:, j * P:(j + 1) * P] for part in (HI, LO))
                        hi_v = (y_bank[:], p_hi, v.rearrange("p s d -> p (s d)"))
                        lo_v = (y_bank[:, 0:D], p_lo, v[:, HI])
                        if g == 0 and j == 0:
                            nc.tensor.matmul(*hi_v, start=True, stop=False)
                            mm = nc.tensor.matmul(*lo_v, start=False, stop=False)
                        else:
                            nc.tensor.matmul(*lo_v, start=False, stop=False)
                            mm = nc.tensor.matmul(*hi_v, start=False, stop=(g == BANKS - 1 and j == TPB - 1))
                    return mm

                def step(par, f, h, n, has_next, more_x, opens, closes):
                    s4 = at(pe, n * 8 + 4 * f)
                    s1 = n * 2 + f
                    has_scores = has_next or not (closes and f == 1)
                    has_q = f == 0 and (has_next or not closes)
                    for g in range(BANKS):
                        if g == 0:
                            pe.wait_ge(exp_done, s1 + 1)
                        if g == 3 and not has_next:
                            pe.wait_ge(pt_lo, s4 + 2)
                        turn(g)
                        if has_scores:
                            if g == 0 and f == 1:
                                pe.wait_ge(q_lo, n + 1)
                                if closes:
                                    pe.wait_ge(k_lo, n + (C + 1))
                            pe.wait_ge(scored, s4 + (g + 1))
                            scores(k_split[1 - par if closes and f == 1 else par], 1 - f, g)
                        if g == 1:
                            pe.wait_ge(pt_lo, s4 + 1)
                            pe.wait_ge(y_added, s1 + 1)
                            if f == 0:
                                pe.wait_ge(v_lo, n + C if has_next else H * C)
                            if f == 0 and closes and more_x:
                                turn_x(pe, par, proj_bank, h * 16 + 48)
                            values(par, 0, has_next)
                            if has_next and f == 1:
                                pe.wait_ge(w_lo["w_v"], n + (C + 1))
                                pe.wait_ge(k_lo, n + (C + 1))
                                project(proj_bank, w_split["w_v"], xt[1 - par]).then_inc(vt_done, 1)
                        if g == 2 and has_next:
                            pe.wait_ge(pt_lo, s4 + 2)
                            values(par, 1, has_next)
                        if g == 3 and not has_next:
                            values(par, 1, has_next)
                    if has_q:
                        pe.wait_ge(w_lo["w_q"], n + 2)
                        if closes and more_x:
                            pe.wait_ge(xt_lo, h + 3)
                        if not has_next:
                            pe.wait_ge(q_lo, n)
                        project(proj_bank, w_split["w_q"], xt[1 - par if closes else par]).then_inc(q_done, 1)
                    pe.wait_ge(pt_lo, s4 + 3)
                    values(par, 2, has_next)
                    if f == 0:
                        pe.wait_ge(pt_lo, s4 + 4)
                        values(par, 3, has_next, range(TPB // 2))
                    if has_next and f == 0:
                        pe.wait_ge(w_lo["w_k"], n + (C + 1))
                        pe.wait_ge(q_lo, n + 1)
                        project(proj_bank, w_split["w_k"], xt[1 - par]).then_inc(k_done, 1)
                    if has_next and f == 1:
                        pe.wait_ge(vt_lo, n + (C + 1))
                        if opens:
                            pe.wait_ge(wout_lo, h + 2)
                        project(proj_bank, vt_split, w_out).then_inc(v_done, 1)
                    if f == 1:
                        pe.wait_ge(pt_lo, s4 + 4)
                    values(par, 3, has_next, range(TPB // 2 if f == 0 else 0, TPB)).then_inc(y_done, 1)

                def block_steps(par, h, c, has_next, more_x, builds):
                    n, opens, closes = place_of(pe, h, c)
                    for f in range(HALVES):
                        step(par, f, h, n, has_next, more_x, opens, closes)

                heads(pe, block_steps)

            @block.gpsimd
            def _(pool):
                def block_steps(par, h, c, has_next, more_x, builds):
                    n, opens, closes = place_of(pool, h, c)
                    if has_next or not closes:
                        lo_w(pool, "w_q", raw["w_q"][:], n + 2)
                    if has_next:
                        lo_w(pool, "w_k", raw["w_k"][:], n + (C + 1))
                        lo_w(pool, "w_v", raw["w_v"][:], n + (C + 1))
                    if has_next and opens:
                        lo_wout(pool, h + 2)

                heads(pool, block_steps)

                pool.wait_ge(ln_step, 5)
                for t in range(NORM_FIRST, NORM_LAST):
                    normalise_tile(nc.gpsimd, t).then_inc(normed_by_pool, 1)

            @block.scalar
            def _(act):
                def sqrt_of(part, tiles):
                    act.wait_ge(ln_var, part + 1)
                    nc.scalar.activation(std[:, tiles], var_eps[:, tiles], ACT.Sqrt).then_inc(ln_std, 1)

                def block_steps(par, h, c, has_next, more_x, builds):
                    n, opens, closes = place_of(act, h, c)

                    def hi_next(name, used, uses):
                        hi_w(act, name, raw[name][:], raw_loaded[name], n * 16 + 16, used, uses)

                    for f in range(HALVES):
                        s4 = at(act, n * 8 + 4 * f)
                        for g in range(BANKS):
                            hi_of(act, turned, s4 + (g + 1), pt_group(HI, g, not has_next), pt_bank[g % 2][:], pt_hi)
                            if f == 0:
                                if g == 0 and (has_next or not closes):
                                    hi_next("w_q", q_done, n + 1)
                                if g == 1 and has_next:
                                    hi_next("w_k", k_done, n + C)
                                if g == 2 and has_next:
                                    hi_next("w_v", vt_done, n + C)
                                if g == 1 and closes and more_x:
                                    hi_of(act, xt_turned, h + 3, xt[par][:, HI], halves(proj_bank), xt_hi)
                                if g == 3 and opens and has_next:
                                    hi_wout(act, h + 2)
                            if g == 3 and closes and f == 1 and not has_next:
                                sqrt_of(0, slice(0, TILES - 1))
                            if g == 1 and f == 1 and has_next:
                                hi_of(act, vt_done, n + (C + 1), vt_split[:, HI], halves(proj_bank), vt_hi)
                        if f == 0 and (has_next or not closes):
                            hi_of(act, q_done, n + 2, q_split[:, HI], halves(proj_bank), q_hi, SCALE / 2)
                        if has_next or not (closes and f == 1):
                            exp_tile(act, n * 2 + (f + 2))
                        else:
                            sqrt_of(1, slice(TILES - 1, TILES))
                        if has_next and f == 0:
                            hi_of(act, k_done, n + (C + 1), k_part(k_split[1 - par], HI, c), halves(proj_bank), k_hi)
                        if has_next and f == 1:
                            hi_of(act, v_done, n + (C + 1), v_part(v_split[1 - par], HI, c), halves(proj_bank), v_hi)

                exp_tile(act, 1)
                heads(act, block_steps)

            @block.vector
            def _(dve):
                def moments(t):
                    dve.wait_ge(y_added, (H - 1) * TILES + t + 2)
                    nc.vector.bn_stats(bn, y_acc[:, t, :]).then_inc(bn_ready, 1)
                    dve.wait_ge(bn_ready, t + 1)
                    nc.vector.bn_aggr(mean_var[:, t, :], bn).then_inc(mv_ready, 1)

                def all_vars(part, tiles):
                    dve.wait_ge(mv_ready, tiles.stop)
                    nc.vector.tensor_scalar(var_eps[:, tiles], mean_var[:, tiles, 1], EPS, None,
                                            ALU.add).then_inc(ln_var, 1)

                def inverse_std(part, tiles):
                    dve.wait_ge(ln_std, part + 1)
                    nc.vector.reciprocal(rstd[:, tiles], std[:, tiles]).then_inc(ln_step, 1)
                    dve.wait_ge(ln_step, 5 * part + 1)
                    nc.vector.tensor_tensor(newton[:, tiles], rstd[:, tiles], rstd[:, tiles],
                                            ALU.mult).then_inc(ln_step, 1)
                    dve.wait_ge(ln_step, 5 * part + 2)
                    nc.vector.tensor_tensor(inv[:, tiles], newton[:, tiles], var_eps[:, tiles],
                                            ALU.mult).then_inc(ln_step, 1)
                    dve.wait_ge(ln_step, 5 * part + 3)
                    nc.vector.tensor_scalar(newton[:, tiles], inv[:, tiles], -0.5, 1.5, ALU.mult,
                                            ALU.add).then_inc(ln_step, 1)
                    dve.wait_ge(ln_step, 5 * part + 4)
                    nc.vector.tensor_tensor(inv[:, tiles], newton[:, tiles], rstd[:, tiles],
                                            ALU.mult).then_inc(ln_step, 1)
                    dve.wait_ge(ln_step, 5 * part + 5)

                def normalise(tiles):
                    for t in range(tiles.start, tiles.stop):
                        normalise_tile(nc.vector, t).then_inc(normed, 1)

                def step(par, f, h, n, c, has_next, more_x, builds, opens, closes):
                    s4 = at(dve, n * 8 + 4 * f)
                    s1 = at(dve, n * 2 + f)
                    has_scores = has_next or not (closes and f == 1)
                    v = at(dve, c * HALVES + (f + EARLY_TILES)) if builds else None
                    ends_build = isinstance(h, int) and h == 0 and (
                        not opens or f == 1 if builds else c == BUILD_BLOCKS and f == 0)
                    last_v = at(dve, c * HALVES + (f + EARLY_TILES - 1)) if ends_build else None
                    for g in range(BANKS):
                        if has_scores:
                            dve.wait_ge(scores_done, s4 + (5 + g))
                            dve.wait_ge(m_loaded[g], s1 * 16 + 16)
                        lo_of(dve, pt_hi, s4 + (g + 1), pt_group(LO, g, not has_next), pt_group(HI, g, not has_next),
                              pt_bank[g % 2][:], pt_lo)
                        if has_scores:
                            score(g, c * HALVES + (f + 1))
                        if g == 0:
                            dve.wait_ge(exp_done, s1 + 1)
                            dve.wait_ge(floor_done, s1 + 1)
                            nc.vector.scalar_tensor_tensor(out=denom, in0=floor_exp,
                                                           scalar=count[:, bass.ds(c * HALVES + f, 1)], in1=row_sum,
                                                           op0=ALU.mult, op1=ALU.add).then_inc(denom_ready, 1)
                            dve.wait_ge(denom_ready, s1 + 1)
                            nc.vector.reciprocal(rdenom, denom).then_inc(rdenom_ready, 1)
                        if g == 0 and not has_next and not (opens and f == 0):
                            moments(c * HALVES + f - 1)
                        if g == 0 and ends_build and not (opens and f == 0):
                            put_chunk(dve, last_v, BANKS - 2)
                        if g == 1 and ends_build:
                            build_chunk(dve, last_v, BANKS - 1)
                        if g == 2 and builds:
                            mark_chunk(dve, v, 0)
                        if not has_scores and g == 1:
                            all_vars(0, slice(0, TILES - 1))
                        if g == 1 and f == 0 and closes and more_x:
                            lo_of(dve, xt_hi, h + 3, xt[par][:, LO], xt[par][:, HI], halves(proj_bank), xt_lo)
                        if g == 1 and f == 1 and has_next:
                            lo_of(dve, vt_hi, n + (C + 1), vt_split[:, LO], vt_split[:, HI],
                                  halves(proj_bank), vt_lo)
                    if has_scores:
                        row_max(dve, s4 + 8, s1 + 2)
                    else:
                        inverse_std(0, slice(0, TILES - 1))
                        normalise(slice(0, NORM_FIRST))
                    if f == 0 and (has_next or not closes):
                        lo_of(dve, q_hi, n + 2, q_split[:, LO], q_split[:, HI], halves(proj_bank), q_lo, SCALE / 2)
                    if builds:
                        for q in range(BANKS - 2):
                            put_chunk(dve, v, q)
                            mark_chunk(dve, v, q + 1)
                    if has_next and f == 0:
                        lo_of(dve, k_hi, n + (C + 1), k_part(k_split[1 - par], LO, c), k_part(k_split[1 - par], HI, c),
                              halves(proj_bank), k_lo)
                    tile = c * HALVES + f
                    y = y_acc[:, tile, :] if isinstance(tile, int) else \
                        y_acc[:, bass.ds(tile, 1), :].rearrange("p a d -> p (a d)")
                    if isinstance(h, int) and h == 0 and opens:
                        dve.wait_ge(y_init, 32)
                    dve.wait_ge(y_done, s1 + 1)
                    dve.wait_ge(rdenom_ready, s1 + 1)
                    nc.vector.scalar_tensor_tensor(out=y, in0=y_bank[:, 0:D], scalar=rdenom, in1=y,
                                                   op0=ALU.mult, op1=ALU.add).then_inc(y_half, 1)
                    dve.wait_ge(y_half, s1 + 1)
                    nc.vector.scalar_tensor_tensor(out=y, in0=y_bank[:, D:2 * D], scalar=rdenom, in1=y,
                                                   op0=ALU.mult, op1=ALU.add).then_inc(y_added, 1)
                    if has_next and f == 1:
                        lo_of(dve, v_hi, n + (C + 1), v_part(v_split[1 - par], LO, c), v_part(v_split[1 - par], HI, c),
                              halves(proj_bank), v_lo)

                def block_steps(par, h, c, has_next, more_x, builds):
                    n, opens, closes = place_of(dve, h, c)
                    for f in range(HALVES):
                        step(par, f, h, n, c, has_next, more_x, builds, opens, closes)

                for q in range(BANKS - LATE_CHUNKS, BANKS):
                    build_chunk(dve, EARLY_TILES - 1, q)
                heads(dve, block_steps, unroll_last=True)

                moments(TILES - 1)
                all_vars(1, slice(TILES - 1, TILES))
                normalise(slice(NORM_LAST, TILES - 1))
                inverse_std(1, slice(TILES - 1, TILES))
                normalise(slice(TILES - 1, TILES))


_INS = ["x", "adj", "L0_gnn_Wq", "L0_gnn_Wk", "L0_gnn_Wv", "L0_gnn_Wout"]


def kernel(**inputs):
    import numpy as _np
    import concourse.bacc as _bacc
    from concourse.bass_utils import run_bass_kernel_spmd as _run

    nc = _bacc.Bacc("TRN2", target_bir_lowering=False, num_devices=1)
    arrays, args = {}, []
    for name in _INS:
        a = _np.ascontiguousarray(inputs[name])
        arrays[f"in_{name}_dram"] = a
        args.append(nc.dram_tensor(f"in_{name}_dram", a.shape, mybir.dt.from_np(a.dtype), kind="ExternalInput").ap())
    args.append(nc.dram_tensor("out_0_dram", inputs["x"].shape, F32, kind="ExternalOutput").ap())
    graph_attention_layernorm(nc, *args)
    r = _run(nc, [arrays], core_ids=[0])
    return r.results[0]["out_0_dram"]
```
